# Optimizing a Trainium2 kernel written in Bass

```python
import numpy as np
import jax
import jax.numpy as jnp

def _softmax(x, axis=-1):
    return jax.nn.softmax(x, axis=axis)

def _gelu(x):
    return jax.nn.gelu(x, approximate=True)

def _silu(x):
    return jax.nn.silu(x)

def _sigmoid(x):
    return jax.nn.sigmoid(x)

def _layernorm(x, axis=-1, eps=1e-05):
    m = jnp.mean(x, axis=axis, keepdims=True)
    v = jnp.var(x, axis=axis, keepdims=True)
    return (x - m) / jnp.sqrt(v + eps)

def _scatter_add(tgt, idx, src, axis=0):
    return tgt.at[idx].add(src)

def _segment_sum(src, seg, n):
    return jax.ops.segment_sum(src, seg, n)
kernel_name = 'mk_sandwich_d1_jaxref_r8_daafd8'

def setup_inputs(seed: int=0):
    np.random.seed(seed)
    _w = jnp.asarray

    def _L0_attn_setup():
        import jax, jax.numpy as jnp
        import numpy as np
        from functools import partial
        D_MODEL = 128
        D_STATE = 16
        D_CONV = 4
        EXPAND = 2
        D_INNER = EXPAND * D_MODEL
        DT_RANK = (D_MODEL + 15) // 16
        BATCH, SEQ = (2, 128)

        def _mamba_params(key):
            ks = jax.random.split(key, 9)
            s = lambda k, shape, scale: jax.random.normal(k, shape, jnp.float32) * scale
            return dict(in_w=s(ks[0], (2 * D_INNER, D_MODEL), D_MODEL ** (-0.5)), conv_w=s(ks[1], (D_INNER, 1, D_CONV), D_CONV ** (-0.5)), conv_b=s(ks[2], (D_INNER,), 0.02), xproj_w=s(ks[3], (DT_RANK + 2 * D_STATE, D_INNER), D_INNER ** (-0.5)), dt_w=s(ks[4], (D_INNER, DT_RANK), DT_RANK ** (-0.5)), dt_b=s(ks[5], (D_INNER,), 0.02), A_log=jnp.log(jnp.broadcast_to(jnp.arange(1, D_STATE + 1, dtype=jnp.float32), (D_INNER, D_STATE))), D=jnp.ones((D_INNER,), jnp.float32), out_w=s(ks[8], (D_MODEL, D_INNER), D_INNER ** (-0.5)))

        def _mamba(x, in_w, conv_w, conv_b, xproj_w, dt_w, dt_b, A_log, D, out_w):
            B, L, _ = x.shape
            xz = jnp.einsum('bld,ed->ble', x, in_w)
            u, z = jnp.split(xz, 2, axis=-1)
            u_c = jnp.swapaxes(u, 1, 2)
            u_c = jax.lax.conv_general_dilated(u_c, conv_w, window_strides=(1,), padding=[(D_CONV - 1, 0)], dimension_numbers=('NCH', 'OIH', 'NCH'), feature_group_count=D_INNER)
            u_c = u_c + conv_b[None, :, None]
            u = jax.nn.silu(jnp.swapaxes(u_c, 1, 2))
            x_dbl = jnp.einsum('bld,ed->ble', u, xproj_w)
            dt = jax.nn.softplus(jnp.einsum('blr,dr->bld', x_dbl[..., :DT_RANK], dt_w) + dt_b)
            Bm = x_dbl[..., DT_RANK:DT_RANK + D_STATE]
            Cm = x_dbl[..., DT_RANK + D_STATE:]
            A = -jnp.exp(A_log)
            dA = jnp.exp(dt[..., None] * A)
            dBu = dt[..., None] * Bm[:, :, None, :] * u[..., None]

            def step(h, ins):
                dA_t, dBu_t, C_t = ins
                h = dA_t * h + dBu_t
                y = jnp.einsum('bdn,bn->bd', h, C_t)
                return (h, y)
            h0 = jnp.zeros((B, D_INNER, D_STATE), dA.dtype)
            _, ys = jax.lax.scan(step, h0, (jnp.swapaxes(dA, 0, 1), jnp.swapaxes(dBu, 0, 1), jnp.swapaxes(Cm, 0, 1)))
            y = jnp.swapaxes(ys, 0, 1) + u * D
            y = y * jax.nn.silu(z)
            return jnp.einsum('bld,ed->ble', y, out_w)
        key = jax.random.key(seed)
        kx, kf, kb, kg = jax.random.split(key, 4)
        inp = {'x': jax.random.normal(kx, (BATCH, SEQ, D_MODEL), jnp.float32), 'gamma': jnp.ones((D_MODEL,), jnp.float32), 'beta': jnp.zeros((D_MODEL,), jnp.float32)}
        for pref, k in (('f_', kf), ('b_', kb)):
            for name, val in _mamba_params(k).items():
                inp[pref + name] = val
        return inp
    _L0_attn_in = _L0_attn_setup()

    def _L0_ffn_setup():
        import jax, jax.numpy as jnp
        import numpy as np
        DIM = 128
        HIDDEN = 384
        SCALE = 1.0 / 127.0

        def _dequant(w_int, dtype):
            return w_int.astype(dtype) * jnp.asarray(SCALE, dtype)
        key = jax.random.key(seed)
        k_x, k_g, k_u, k_d = jax.random.split(key, 4)
        x = jax.random.normal(k_x, (4, 256, DIM), dtype=jnp.float32)
        w_gate = jax.random.randint(k_g, (HIDDEN, DIM), -127, 128, dtype=jnp.int32)
        w_up = jax.random.randint(k_u, (HIDDEN, DIM), -127, 128, dtype=jnp.int32)
        w_down = jax.random.randint(k_d, (DIM, HIDDEN), -127, 128, dtype=jnp.int32)
        return {'x': x, 'w_gate': w_gate, 'w_up': w_up, 'w_down': w_down}
    _L0_ffn_in = _L0_ffn_setup()
    _d = {'L0_attn_x': _L0_attn_in['x'], 'L0_attn_gamma': _L0_attn_in['gamma'], 'L0_attn_beta': _L0_attn_in['beta'], 'L0_attn_f_in_w': _L0_attn_in['f_in_w'], 'L0_attn_f_conv_w': _L0_attn_in['f_conv_w'], 'L0_attn_f_conv_b': _L0_attn_in['f_conv_b'], 'L0_attn_f_xproj_w': _L0_attn_in['f_xproj_w'], 'L0_attn_f_dt_w': _L0_attn_in['f_dt_w'], 'L0_attn_f_dt_b': _L0_attn_in['f_dt_b'], 'L0_attn_f_A_log': _L0_attn_in['f_A_log'], 'L0_attn_f_D': _L0_attn_in['f_D'], 'L0_attn_f_out_w': _L0_attn_in['f_out_w'], 'L0_attn_b_in_w': _L0_attn_in['b_in_w'], 'L0_attn_b_conv_w': _L0_attn_in['b_conv_w'], 'L0_attn_b_conv_b': _L0_attn_in['b_conv_b'], 'L0_attn_b_xproj_w': _L0_attn_in['b_xproj_w'], 'L0_attn_b_dt_w': _L0_attn_in['b_dt_w'], 'L0_attn_b_dt_b': _L0_attn_in['b_dt_b'], 'L0_attn_b_A_log': _L0_attn_in['b_A_log'], 'L0_attn_b_D': _L0_attn_in['b_D'], 'L0_attn_b_out_w': _L0_attn_in['b_out_w'], 'L0_ffn_w_gate': _L0_ffn_in['w_gate'], 'L0_ffn_w_up': _L0_ffn_in['w_up'], 'L0_ffn_w_down': _L0_ffn_in['w_down']}
    _x0 = _d['L0_attn_x']
    _d['L0_attn_x'] = jax.random.normal(jax.random.fold_in(jax.random.key(seed), 1), (4, 512, 128), dtype=_x0.dtype)
    del _x0
    return _d

def reference(L0_attn_x, L0_attn_gamma, L0_attn_beta, L0_attn_f_in_w, L0_attn_f_conv_w, L0_attn_f_conv_b, L0_attn_f_xproj_w, L0_attn_f_dt_w, L0_attn_f_dt_b, L0_attn_f_A_log, L0_attn_f_D, L0_attn_f_out_w, L0_attn_b_in_w, L0_attn_b_conv_w, L0_attn_b_conv_b, L0_attn_b_xproj_w, L0_attn_b_dt_w, L0_attn_b_dt_b, L0_attn_b_A_log, L0_attn_b_D, L0_attn_b_out_w, L0_ffn_w_gate, L0_ffn_w_up, L0_ffn_w_down):

    def _L0_attn_ref(x, gamma, beta, f_in_w, f_conv_w, f_conv_b, f_xproj_w, f_dt_w, f_dt_b, f_A_log, f_D, f_out_w, b_in_w, b_conv_w, b_conv_b, b_xproj_w, b_dt_w, b_dt_b, b_A_log, b_D, b_out_w):
        import jax, jax.numpy as jnp
        import numpy as np
        from functools import partial
        D_MODEL = 128
        D_STATE = 16
        D_CONV = 4
        EXPAND = 2
        D_INNER = EXPAND * D_MODEL
        DT_RANK = (D_MODEL + 15) // 16
        BATCH, SEQ = (2, 128)

        def _mamba_params(key):
            ks = jax.random.split(key, 9)
            s = lambda k, shape, scale: jax.random.normal(k, shape, jnp.float32) * scale
            return dict(in_w=s(ks[0], (2 * D_INNER, D_MODEL), D_MODEL ** (-0.5)), conv_w=s(ks[1], (D_INNER, 1, D_CONV), D_CONV ** (-0.5)), conv_b=s(ks[2], (D_INNER,), 0.02), xproj_w=s(ks[3], (DT_RANK + 2 * D_STATE, D_INNER), D_INNER ** (-0.5)), dt_w=s(ks[4], (D_INNER, DT_RANK), DT_RANK ** (-0.5)), dt_b=s(ks[5], (D_INNER,), 0.02), A_log=jnp.log(jnp.broadcast_to(jnp.arange(1, D_STATE + 1, dtype=jnp.float32), (D_INNER, D_STATE))), D=jnp.ones((D_INNER,), jnp.float32), out_w=s(ks[8], (D_MODEL, D_INNER), D_INNER ** (-0.5)))

        def _mamba(x, in_w, conv_w, conv_b, xproj_w, dt_w, dt_b, A_log, D, out_w):
            B, L, _ = x.shape
            xz = jnp.einsum('bld,ed->ble', x, in_w)
            u, z = jnp.split(xz, 2, axis=-1)
            u_c = jnp.swapaxes(u, 1, 2)
            u_c = jax.lax.conv_general_dilated(u_c, conv_w, window_strides=(1,), padding=[(D_CONV - 1, 0)], dimension_numbers=('NCH', 'OIH', 'NCH'), feature_group_count=D_INNER)
            u_c = u_c + conv_b[None, :, None]
            u = jax.nn.silu(jnp.swapaxes(u_c, 1, 2))
            x_dbl = jnp.einsum('bld,ed->ble', u, xproj_w)
            dt = jax.nn.softplus(jnp.einsum('blr,dr->bld', x_dbl[..., :DT_RANK], dt_w) + dt_b)
            Bm = x_dbl[..., DT_RANK:DT_RANK + D_STATE]
            Cm = x_dbl[..., DT_RANK + D_STATE:]
            A = -jnp.exp(A_log)
            dA = jnp.exp(dt[..., None] * A)
            dBu = dt[..., None] * Bm[:, :, None, :] * u[..., None]

            def step(h, ins):
                dA_t, dBu_t, C_t = ins
                h = dA_t * h + dBu_t
                y = jnp.einsum('bdn,bn->bd', h, C_t)
                return (h, y)
            h0 = jnp.zeros((B, D_INNER, D_STATE), dA.dtype)
            _, ys = jax.lax.scan(step, h0, (jnp.swapaxes(dA, 0, 1), jnp.swapaxes(dBu, 0, 1), jnp.swapaxes(Cm, 0, 1)))
            y = jnp.swapaxes(ys, 0, 1) + u * D
            y = y * jax.nn.silu(z)
            return jnp.einsum('bld,ed->ble', y, out_w)
        res = x
        mu = jnp.mean(x, axis=-1, keepdims=True)
        var = jnp.mean(jnp.square(x - mu), axis=-1, keepdims=True)
        xn = (x - mu) * jax.lax.rsqrt(var + 1e-05) * gamma + beta
        out_fwd = _mamba(xn, f_in_w, f_conv_w, f_conv_b, f_xproj_w, f_dt_w, f_dt_b, f_A_log, f_D, f_out_w)
        out_bwd = _mamba(xn[:, ::-1, :], b_in_w, b_conv_w, b_conv_b, b_xproj_w, b_dt_w, b_dt_b, b_A_log, b_D, b_out_w)[:, ::-1, :]
        return res + out_fwd + out_bwd

    def _L0_ffn_ref(x, w_gate, w_up, w_down):
        import jax, jax.numpy as jnp
        import numpy as np
        DIM = 128
        HIDDEN = 384
        SCALE = 1.0 / 127.0

        def _dequant(w_int, dtype):
            return w_int.astype(dtype) * jnp.asarray(SCALE, dtype)
        wg = _dequant(w_gate, x.dtype)
        wu = _dequant(w_up, x.dtype)
        wd = _dequant(w_down, x.dtype)
        gate = jnp.einsum('bsd,hd->bsh', x, wg)
        up = jnp.einsum('bsd,hd->bsh', x, wu)
        h = jax.nn.silu(gate) * up
        return jnp.einsum('bsh,dh->bsd', h, wd)
    x = L0_attn_x
    x = x + _layernorm(_L0_attn_ref(_layernorm(x, axis=-1), L0_attn_gamma, L0_attn_beta, L0_attn_f_in_w, L0_attn_f_conv_w, L0_attn_f_conv_b, L0_attn_f_xproj_w, L0_attn_f_dt_w, L0_attn_f_dt_b, L0_attn_f_A_log, L0_attn_f_D, L0_attn_f_out_w, L0_attn_b_in_w, L0_attn_b_conv_w, L0_attn_b_conv_b, L0_attn_b_xproj_w, L0_attn_b_dt_w, L0_attn_b_dt_b, L0_attn_b_A_log, L0_attn_b_D, L0_attn_b_out_w), axis=-1)
    x = x + _layernorm(_L0_ffn_ref(_layernorm(x, axis=-1), L0_ffn_w_gate, L0_ffn_w_up, L0_ffn_w_down), axis=-1)
    return x

_drawn_inputs = setup_inputs


def setup_inputs(seed=0):
    import zlib

    import numpy as np

    out = dict(_drawn_inputs(seed))
    spreads = {'L0_attn_gamma': (1.0, 0.2),
     'L0_attn_beta': (0.0, 0.1),
     'L0_attn_f_D': (1.0, 0.2),
     'L0_attn_b_D': (1.0, 0.2)}
    factors = {'L0_attn_f_conv_b': 6.044,
     'L0_attn_f_dt_b': 8.0,
     'L0_attn_b_conv_b': 6.753,
     'L0_attn_b_dt_b': 8.0}
    for name, (base, spread) in spreads.items():
        noise = np.random.default_rng([zlib.crc32(name.encode()), seed]).standard_normal(out[name].shape)
        drawn = base * np.exp(spread * noise) if base else spread * noise
        out[name] = jnp.asarray(drawn.astype(out[name].dtype))
    for name, factor in factors.items():
        out[name] = (out[name] * factor).astype(out[name].dtype)
    return out
```

```python
from contextlib import ExitStack

import concourse.bass as bass
from concourse import mybir

P = 128
BATCH, SEQ, DM = 4, 512, 128
DI, NS, RANK, TAPS = 256, 16, 8, 4
HID = 384
PAIRS = 2
PT = BATCH // PAIRS * SEQ
BLK = PT // P
BPS = SEQ // P
UNITS = 2 * PAIRS
SEGS = 2 * UNITS
STEPS = SEGS * NS
EPS = 1e-5

ROW_HI, ROW_LO, ROW_MID, ROW_DT = 0, 32, 64, 96
XROWS = ROW_DT + RANK
COLS = {}
_at = 0
for _name, _n in (("ident", P), ("rev", P), ("gamma", 1), ("beta", 1), ("conv_b", 4), ("skip", 4),
                  ("a_log", 4 * NS), ("sel", NS), ("wz", 2 * DI), ("wx", 4 * XROWS),
                  ("wo", 4 * DM), ("wdt", 2 * DI)):
    COLS[_name] = (_at, _at + _n)
    _at += _n
NCOLS = _at

DA_RING, H_RING, BB_RING, C_RING = 3, 4, 2, 6

ALU = mybir.AluOpType
ACT = mybir.ActivationFunctionType
F32 = mybir.dt.float32
BF16 = mybir.dt.bfloat16
I32 = mybir.dt.int32


def state_of(i):
    k, h, p = i // (2 * NS), i // NS % 2, i % NS
    return p if (k + h) % 2 == 0 else NS - 1 - p


def plan_c_loads():
    loads, held, last = [], [None] * C_RING, [-1] * C_RING
    for i in range(STEPS):
        key = (i // (2 * NS), state_of(i))
        slot = key[1] % C_RING
        if held[slot] != key:
            loads.append((key[0], key[1], slot, i, last[slot]))
            held[slot] = key
        last[slot] = i
    return loads


def plan():
    at = {i: [] for i in range(-1, STEPS + 3)}

    def put(slot, *items):
        at[slot].extend(items)

    def norm(slots, w, q):
        for slot, stage in zip(slots, ("ln_stats", "ln_pow", "ln_shift", "ln_apply")):
            put(slot, (stage, w, q))

    def ffn(slot, q, s, pace):
        for c in range(3):
            put(slot(c), ("ffn_gate", q, s, c))
        put(slot(3), ("ffn_silu", q, s))
        for c in range(3):
            put(slot(4 + c), ("ffn_up", q, s, c))
        put(slot(7), ("ffn_down", q, s))

    pre = -1
    norm([pre] * 4, 0, 0)
    norm([pre] * 4, 1, 0)
    put(pre, ("turn", 0, 0, 0), ("turn", 0, 0, 1))
    for h in range(2):
        for s in range(2):
            put(pre, *[("tap", 0, h, s, t) for t in range(TAPS)], ("conv_out", 0, h, s))
    put(pre, ("silu_u", 0), ("xproj", 0, 0), ("xproj", 0, 1), ("split", 0))
    for h in range(2):
        for s in range(2):
            put(pre, ("dt", 0, h, s))
    put(pre, ("sp_exp", 0), ("sp_rest", 0, 0), ("sp_rest", 0, 1), ("sp_ln", 0, 0), ("sp_ln", 0, 1),
        ("dtu", 0, 0), ("skip", 0, 0), ("dtu", 0, 1), ("skip", 0, 1))
    put(pre, ("turn", 0, 1, 0), ("turn", 0, 1, 1))

    for k in range(UNITS):
        o, q, kn = 2 * NS * k, k // 2, k + 1
        for n, (h, s) in enumerate(((0, 0), (0, 1), (1, 0), (1, 1))):
            put(o + 4 + 2 * n, ("z", k, h, s))
        if kn < UNITS:
            if k % 2:
                put(o, ("turn", q + 1, 0, 0))
                put(o + 1, ("turn", q + 1, 0, 1))
                put(o + 25, ("turn", q + 1, 1, 0))
                put(o + 26, ("turn", q + 1, 1, 1))
            elif q + 1 < PAIRS:
                norm([o + 25, o + 25, o + 26, o + 27], 0, q + 1)
                norm([o + 28, o + 28, o + 29, o + 30], 1, q + 1)
            taps = [("tap", kn, h, s, t) for h in range(2) for s in range(2) for t in range(TAPS)]
            for n, tap in enumerate(taps):
                put(o + 3 + n // 2, tap)
                if tap[4] == TAPS - 1:
                    put(o + 3 + n // 2, ("conv_out", kn, tap[2], tap[3]))
            put(o + 12, ("silu_u", kn))
        put(o + 12, ("silu_z", k))
        if kn < UNITS:
            put(o + 13, ("xproj", kn, 0))
            put(o + 14, ("xproj", kn, 1))
            put(o + 15, ("split", kn))
            put(o + 15, ("dt", kn, 0, 0))
            put(o + 16, ("dt", kn, 0, 1), ("dt", kn, 1, 0))
            put(o + 17, ("dt", kn, 1, 1))
            put(o + 18, ("sp_exp", kn))
            put(o + 19, ("sp_rest", kn, 0))
            put(o + 20, ("sp_rest", kn, 1))
            put(o + 21, ("sp_ln", kn, 0), ("sp_ln", kn, 1))
            put(o + 22, ("dtu", kn, 0))
            put(o + 23, ("dtu", kn, 1), ("skip", kn, 0))
            put(o + 24, ("skip", kn, 1))

    o = 2 * NS * 2
    put(o + 3, ("oproj", 0, 0))
    put(o + 4, ("oproj", 0, 1))
    norm([o + 5, o + 5, o + 6, o + 7], 2, 0)
    put(o + 8, ("add_attn", 0))
    o = 2 * NS * 3
    norm([o + 1, o + 1, o + 2, o + 3], 3, 0)
    put(o + 5, ("turn_x1", 0, 0))
    put(o + 6, ("turn_x1", 0, 1))
    ffn(lambda n: o + 7 + n, 0, 0, 1)
    ffn(lambda n: o + 16 + n, 0, 1, 1)
    norm([o + 25, o + 25, o + 26, o + 27], 4, 0)
    put(o + 29, ("add_ffn", 0))

    end = STEPS + 2
    tail = [("oproj", 1, 0), ("oproj", 1, 1)]
    tail += [(x, 2, 1) for x in ("ln_stats", "ln_pow", "ln_shift", "ln_apply")] + [("add_attn", 1)]
    tail += [(x, 3, 1) for x in ("ln_stats", "ln_pow", "ln_shift", "ln_apply")]
    tail += [("turn_x1", 1, 0), ("turn_x1", 1, 1)]

    order = []
    for i in range(-1, STEPS + 3):
        if i == -1:
            order += at[-1] + [("exp", 0), ("exp", 1), ("bcast", 0), ("bcast", 1)]
            continue
        if i < STEPS:
            order += [("scan", i), ("mul_c", i)]
            if i + 1 < STEPS and i >= 1:
                order.append(("bcast", i + 1))
            if i + 2 < STEPS:
                order.append(("exp", i + 2))
        if i >= 2 and i - 2 < STEPS:
            f = i - 2
            if f % NS == 0:
                order.append(("seed", f // NS))
            order.append(("fold", f))
            if f % NS == NS - 1:
                order += [("y_out", f // NS), ("back", f // NS, 0), ("back", f // NS, 1)]
        order += at[i]
    at_end = {}
    ffn(lambda n: end, 1, 0, 0)
    ffn(lambda n: end, 1, 1, 0)
    order += tail + at[end][-16:]
    order += [(x, 4, 1) for x in ("ln_stats", "ln_pow", "ln_shift", "ln_apply")] + [("add_ffn", 1)]
    return order


SCRATCH = ("turn", "conv_out", "z", "xproj", "dt", "back", "oproj", "turn_x1", "ffn_gate", "ffn_up",
           "ffn_down")


def plan_banks(order):
    banks, count = {}, [0, 0]
    first = order.index(("scan", 0))
    last = max(n for n, x in enumerate(order) if x[0] == "back")
    open_use = None
    turn = 0
    for n, x in enumerate(order):
        if x[0] not in SCRATCH and x[0] != "tap":
            continue
        if first < n <= last:
            b = 0 if x[0] in ("tap", "conv_out") else 1
        else:
            if x[0] == "conv_out" or (x[0] == "tap" and x[4] > 0):
                b = turn
            else:
                turn = 1 - turn
                b = turn
        if x[0] == "tap":
            if x[4] == 0:
                count[b] += 1
                banks[("conv_out",) + x[1:4]] = (b, count[b])
            continue
        if x[0] == "conv_out":
            continue
        count[b] += 1
        banks[x] = (b, count[b])
    return banks


def mamba_sandwich(nc, x, packed, conv_taps, w_u, w_ffn, c_rows, out):
    ORDER = plan()
    BANK = plan_banks(ORDER)
    C_LOADS = plan_c_loads()
    c_need, c_count = {}, [0] * C_RING
    for k, n, slot, step, _ in C_LOADS:
        c_count[slot] += 1
        c_need[step] = (slot, 16 * c_count[slot])

    with ExitStack() as ctx:
        def sb(name, shape, dt=F32):
            return ctx.enter_context(nc.sbuf_tensor(name, shape, dt))

        def sem(name):
            return ctx.enter_context(nc.semaphore(name))

        bb = ctx.enter_context(nc.psum_tensor("bb", [P, BB_RING, PT], F32))
        ysum = ctx.enter_context(nc.psum_tensor("ysum", [P, PT], F32))
        scr = ctx.enter_context(nc.psum_tensor("scr", [P, 2, SEQ], F32))

        wts = sb("wts", [P, NCOLS])
        wconv = sb("wconv", [P, 2, TAPS, DI])
        neg_a = sb("neg_a", [P, 4 * NS])
        sel = sb("sel", [ROW_DT, NS, P], BF16)
        wffn = sb("wffn", [P, 3 * HID])
        stats = sb("stats", [P, 5, PAIRS, BLK, 6])
        mean_var = sb("mean_var", [P, 5, PAIRS, BLK, 2])
        rstd = sb("rstd", [P, 5, PAIRS, BLK])
        shift = sb("shift", [P, 5, PAIRS, BLK])
        minus_half = sb("minus_half", [P, BLK])
        x0 = sb("x0", [P, BLK, DM])
        attn_in = sb("attn_in", [P, PAIRS, BLK, DM])
        normed = sb("normed", [P, BLK, DM])
        x1 = sb("x1", [P, BLK, DM])
        o = sb("o", [P, BLK, DM])
        PAD = TAPS - 1
        xn_fwd = sb("xn_fwd", [P, PAIRS, 2, PAD + SEQ])
        xn_rev = sb("xn_rev", [P, 2, PAD + SEQ])
        u = sb("u", [P, 2, PT])
        zs = sb("zs", [P, 2, PT])
        skip = sb("skip", [P, 2, PT])
        parts = sb("parts", [ROW_DT, 2, PT], BF16)
        xdbl = sb("xdbl", [P, PT])
        dt = sb("dt", [P, 3, PT])
        dtu = sb("dtu", [P, 3, PT])
        work = sb("work", [P, 3 * PT])
        da = sb("da", [P, DA_RING, 2, SEQ])
        hq = sb("hq", [P, H_RING, PT])
        c_tiles = sb("c_tiles", [P, C_RING, PT])
        y_t = sb("y_t", [P, PT])
        gated = sb("gated", [P, 2, 2, PT])

        e = work[:, 0:2 * PT].rearrange("p (h t) -> p h t", h=2)
        tmp = work[:, 2 * PT:3 * PT]
        x1_t = work[:, 0:PT]
        hid = work[:, PT:PT + 3 * SEQ].rearrange("p (c t) -> p c t", c=3)
        rest = tmp
        mid_lo = xdbl[ROW_LO:ROW_LO + 32, 0:PT // 2].bitcast(BF16)
        w_u_stage = hq[:, 0, 0:2 * DI].rearrange("p (d e) -> p d e", d=2)
        ffn_stage = hq[:, 1:3, :].rearrange("p a b -> p (a b)")[:, 0:3 * HID].bitcast(I32)

        def col(name):
            return wts[:, COLS[name][0]:COLS[name][1]]

        ident, rev = col("ident"), col("rev")
        wz = col("wz").rearrange("p (d e) -> p d e", d=2)
        wx = col("wx").rearrange("p (d h r) -> p d h r", d=2, h=2)
        wo = col("wo").rearrange("p (d h m) -> p d h m", d=2, h=2)
        wdt = col("wdt").rearrange("p (d e) -> p d e", d=2)
        perm = [ident, rev]
        w_gate, w_up, w_down = (wffn[:, n * HID:(n + 1) * HID] for n in range(3))

        def vec(name, d, h):
            c = COLS[name][0] + 2 * d + h
            return wts[:, c:c + 1]

        s_x0 = sem("x0_loaded")
        s_x1in = sem("x1_holds_x0")
        s_w = sem("packed_loaded")
        s_wc = sem("conv_taps_loaded")
        s_wf = sem("ffn_weights_loaded")
        s_zero = sem("zeros_set")
        s_wconv = sem("conv_folded")
        s_wffn = sem("ffn_dequantised")
        s_expa = sem("exp_a_log_done")
        s_nega = sem("neg_a_done")
        s_sel = sem("selector_done")
        s_full = [sem("scratch0_written"), sem("scratch1_written")]
        s_read = [sem("scratch0_read"), sem("scratch1_read")]
        s_bcast = sem("b_broadcast")
        s_dbu = sem("dbu_done")
        s_exp = sem("da_done")
        s_scan = sem("scan_done")
        s_q = sem("c_product_done")
        s_fold = sem("state_summed")
        s_seed = sem("skip_seeded")
        s_yout = sem("y_copied")
        s_cl = [sem(f"c_tile{n}_loaded") for n in range(C_RING)]
        s_cst = sem("c_rows_stored")
        s_xread = sem("xdbl_rows_copied")
        s_mid = sem("middle_parts_done")
        s_parts = sem("b_parts_done")
        s_silu_u = sem("u_silu_done")
        s_silu_z = sem("z_silu_done")
        s_spexp = sem("softplus_exp_done")
        s_sprest = sem("softplus_rest_done")
        s_spln = sem("softplus_ln_done")
        s_dt = sem("dt_done")
        s_dtu = sem("dtu_done")
        s_skip = sem("skip_done")
        s_stat = [sem(f"ln{w}_stats_done") for w in range(5)]
        s_var = [sem(f"ln{w}_var_done") for w in range(5)]
        s_pow = [sem(f"ln{w}_rstd_done") for w in range(5)]
        s_shift = [sem(f"ln{w}_shift_done") for w in range(5)]
        s_norm = [sem(f"ln{w}_applied") for w in range(5)]
        s_x1 = sem("x1_done")
        s_hsilu = sem("gate_silu_done")
        s_x2 = sem("x2_done")
        s_out = sem("out_stored")
        s_own = sem("dve_own_step")
        s_own_act = sem("softplus_abs_done")
        s_ones = sem("ones_row_set")
        s_half = sem("minus_half_set")

        x_tok = x.rearrange("(q r s) (b p) m -> q p (r s b) m", q=PAIRS, r=1, p=P) if False else \
            x.rearrange("s (b p) m -> p s b m", p=P)
        out_tok = out.rearrange("s (b p) m -> p s b m", p=P)

        def pair_of(ap, q):
            return ap[:, 2 * q:2 * q + 2, :, :]

        def by_seq(tile):
            return tile.rearrange("p (s b) m -> p s b m", s=2)

        def scratch(stage):
            return scr[:, BANK[stage][0], :]

        def may_write(eng, stage):
            b, n = BANK[stage]
            if n > 1:
                eng.wait_ge(s_read[b], n - 1)

        def written(eng, stage):
            b, n = BANK[stage]
            eng.wait_ge(s_full[b], n)

        def was_read(eng, stage):
            b, n = BANK[stage]
            eng.wait_ge(s_read[b], n)

        def tok(s, n=1):
            return slice(s * SEQ, (s + n) * SEQ)

        LN_IN = [lambda q: x0, lambda q: attn_in[:, q], lambda q: o, lambda q: x1, lambda q: o]
        LN_OUT = [lambda q: attn_in[:, q], lambda q: normed, lambda q: normed, lambda q: normed,
                  lambda q: normed]

        block = ctx.enter_context(nc.Block())

        @block.sync
        def _(sp):
            sp.dma_start(by_seq(x0[:]), pair_of(x_tok, 0)).then_inc(s_x0, 16)
            sp.dma_start(wts[:], packed).then_inc(s_w, 16)
            sp.dma_start(w_u_stage, w_u).then_inc(s_wc, 16)
            sp.dma_start(wconv[:], conv_taps).then_inc(s_wc, 16)
            sp.dma_start(ffn_stage, w_ffn).then_inc(s_wf, 16)
            sp.dma_start(by_seq(x1[:]), pair_of(x_tok, 0)).then_inc(s_x1in, 16)
            sp.wait_ge(s_norm[0], 1)
            sp.dma_start(by_seq(x0[:]), pair_of(x_tok, 1)).then_inc(s_x0, 16)
            stored = -1
            last_out = False
            for k, n, slot, step, free in C_LOADS:
                if k > stored:
                    sp.wait_ge(s_xread, 6 * (k + 1))
                    sp.dma_start(c_rows[k], xdbl[NS:2 * NS, :]).then_inc(s_cst, 16)
                    sp.wait_ge(s_cst, 16 * (k + 1))
                    stored = k
                if free >= 0:
                    sp.wait_ge(s_q, free + 1)
                sp.dma_start(c_tiles[:, slot, :], c_rows[k, n].partition_broadcast(P)).then_inc(s_cl[slot], 16)
            sp.wait_ge(s_x2, 1)
            sp.dma_start(pair_of(out_tok, 0), by_seq(o[:])).then_inc(s_out, 16)
            sp.dma_start(by_seq(x1[:]), pair_of(x_tok, 1)).then_inc(s_x1in, 16)
            sp.wait_ge(s_x2, 2)
            sp.wait_ge(s_out, 16)
            sp.dma_start(pair_of(out_tok, 1), by_seq(o[:])).then_inc(s_out, 16)
            sp.wait_ge(s_out, 32)

        @block.tensor
        def _(pe):
            pe.wait_ge(s_w, 16)
            for x_ in ORDER:
                stage, a = x_[0], x_[1:]
                if stage == "bcast":
                    i, = a
                    k = i // (2 * NS)
                    if i == 0:
                        pe.wait_ge(s_sel, 1)
                    if i % (2 * NS) == 0:
                        pe.wait_ge(s_parts, k + 1)
                    if i >= BB_RING:
                        pe.wait_ge(s_scan, i - BB_RING + 1)
                    n = state_of(i)
                    for s in range(2):
                        mm = nc.tensor.matmul(bb[:, i % BB_RING, tok(s)], sel[:, n, :], parts[:, k % 2, tok(s)],
                                              start=True, stop=True)
                    mm.then_inc(s_bcast, 1)
                elif stage == "seed":
                    j, = a
                    pe.wait_ge(s_skip, j + 1)
                    if j >= 1:
                        pe.wait_ge(s_yout, j)
                    for b in range(BLK):
                        mm = nc.tensor.matmul(ysum[:, b * P:(b + 1) * P], skip[:, j % 2, b * P:(b + 1) * P],
                                              ident, start=(b % BPS == 0), stop=False, is_transpose=True,
                                              skip_group_check=True)
                    mm.then_inc(s_seed, 1)
                elif stage == "fold":
                    i, = a
                    pe.wait_ge(s_q, i + 1)
                    for b in range(BLK):
                        mm = nc.tensor.matmul(ysum[:, b * P:(b + 1) * P], hq[:, i % H_RING, b * P:(b + 1) * P],
                                              ident, start=False, stop=(i % NS == NS - 1), is_transpose=True,
                                              skip_group_check=True)
                    mm.then_inc(s_fold, 1)
                elif stage == "back":
                    j, s = a
                    pe.wait_ge(s_yout, j + 1)
                    may_write(pe, x_)
                    d = j // 2 % 2
                    for b in range(BPS):
                        src = s * BPS + (BPS - 1 - b if d else b)
                        mm = nc.tensor.matmul(scratch(x_)[:, b * P:(b + 1) * P], y_t[:, src * P:(src + 1) * P],
                                              perm[d], start=True, stop=True, is_transpose=True)
                    mm.then_inc(s_full[BANK[x_][0]], 1)
                elif stage == "turn":
                    q, d, s = a
                    pe.wait_ge(s_norm[1], q + 1)
                    may_write(pe, x_)
                    for b in range(BPS):
                        src = s * BPS + (BPS - 1 - b if d else b)
                        mm = nc.tensor.matmul(scratch(x_)[:, b * P:(b + 1) * P], normed[:, src, :],
                                              perm[d], start=True, stop=True, is_transpose=True)
                    mm.then_inc(s_full[BANK[x_][0]], 1)
                elif stage == "tap":
                    k, h, s, t = a
                    q, d = k // 2, k % 2
                    use = ("conv_out", k, h, s)
                    if t == 0:
                        pe.wait_ge(s_wconv, 1)
                        pe.wait_ge(s_zero, 1)
                        was_read(pe, ("turn", q, d, s))
                        may_write(pe, use)
                    src = xn_rev[:, s, t:t + SEQ] if d else xn_fwd[:, q, s, t:t + SEQ]
                    mm = nc.tensor.matmul(scratch(use), wconv[:, d, t, h * P:(h + 1) * P], src,
                                          start=(t == 0), stop=(t == TAPS - 1))
                    if t == TAPS - 1:
                        mm.then_inc(s_full[BANK[use][0]], 1)
                elif stage == "z":
                    k, h, s = a
                    q, d = k // 2, k % 2
                    was_read(pe, ("turn", q, 0, s))
                    may_write(pe, x_)
                    nc.tensor.matmul(scratch(x_), wz[:, d, h * P:(h + 1) * P], xn_fwd[:, q, s, PAD:PAD + SEQ],
                                     start=True, stop=True).then_inc(s_full[BANK[x_][0]], 1)
                elif stage == "xproj":
                    k, s = a
                    pe.wait_ge(s_silu_u, k + 1)
                    may_write(pe, x_)
                    for h in range(2):
                        mm = nc.tensor.matmul(scratch(x_)[0:XROWS, :], wx[:, k % 2, h, :], u[:, h, tok(s)],
                                              start=(h == 0), stop=(h == 1))
                    mm.then_inc(s_full[BANK[x_][0]], 1)
                elif stage == "dt":
                    k, h, s = a
                    pe.wait_ge(s_xread, 6 * (k + 1))
                    pe.wait_ge(s_ones, 1)
                    may_write(pe, x_)
                    rows = slice(ROW_DT, XROWS + 1)
                    nc.tensor.matmul(scratch(x_), wdt[rows, k % 2, h * P:(h + 1) * P], xdbl[rows, tok(s)],
                                     start=True, stop=True).then_inc(s_full[BANK[x_][0]], 1)
                elif stage == "oproj":
                    q, s = a
                    for t in range(2):
                        was_read(pe, ("back", 4 * q + 3, t))
                    may_write(pe, x_)
                    for b in range(BPS):
                        at = slice((s * BPS + b) * P, (s * BPS + b + 1) * P)
                        for n in range(4):
                            mm = nc.tensor.matmul(scratch(x_)[:, b * P:(b + 1) * P], gated[:, n // 2, n % 2, at],
                                                  wo[:, n // 2, n % 2, :], start=(b == 0 and n == 0), stop=(n == 3),
                                                  skip_group_check=True)
                    mm.then_inc(s_full[BANK[x_][0]], 1)
                elif stage == "turn_x1":
                    q, s = a
                    pe.wait_ge(s_norm[3], q + 1)
                    may_write(pe, x_)
                    for b in range(BPS):
                        mm = nc.tensor.matmul(scratch(x_)[:, b * P:(b + 1) * P], normed[:, s * BPS + b, :],
                                              ident, start=True, stop=True, is_transpose=True)
                    mm.then_inc(s_full[BANK[x_][0]], 1)
                elif stage in ("ffn_gate", "ffn_up"):
                    q, s, c = a
                    if c == 0 and stage == "ffn_gate":
                        pe.wait_ge(s_wffn, 1)
                        was_read(pe, ("turn_x1", q, s))
                    may_write(pe, x_)
                    w = w_gate if stage == "ffn_gate" else w_up
                    nc.tensor.matmul(scratch(x_), w[:, c * P:(c + 1) * P], x1_t[:, tok(s)],
                                     start=True, stop=True).then_inc(s_full[BANK[x_][0]], 1)
                elif stage == "ffn_down":
                    q, s = a
                    for c in range(3):
                        was_read(pe, ("ffn_up", q, s, c))
                    may_write(pe, x_)
                    for b in range(BPS):
                        for c in range(3):
                            mm = nc.tensor.matmul(scratch(x_)[:, b * P:(b + 1) * P], hid[:, c, b * P:(b + 1) * P],
                                                  w_down[:, c * P:(c + 1) * P], start=(b == 0 and c == 0),
                                                  stop=(c == 2), skip_group_check=True)
                    mm.then_inc(s_full[BANK[x_][0]], 1)

        @block.scalar
        def _(act):
            act.wait_ge(s_w, 16)
            nc.scalar.activation(neg_a[:], col("a_log"), ACT.Exp).then_inc(s_expa, 1)
            for x_ in ORDER:
                stage, a = x_[0], x_[1:]
                if stage == "exp":
                    i, = a
                    j = i // NS
                    if i == 0:
                        act.wait_ge(s_nega, 1)
                        act.wait_ge(s_zero, 1)
                    if i % NS == 0:
                        act.wait_ge(s_dt, j + 1)
                    if i >= DA_RING:
                        act.wait_ge(s_scan, i - DA_RING + 1)
                    c = (j % 4) * NS + state_of(i)
                    nc.scalar.activation(da[:, i % DA_RING, :, 1:SEQ],
                                         dt[:, j % 3, :].rearrange("p (s t) -> p s t", s=2)[:, :, 1:SEQ],
                                         ACT.Exp, scale=neg_a[:, c:c + 1]).then_inc(s_exp, 1)
                elif stage == "y_out":
                    j, = a
                    act.wait_ge(s_fold, NS * (j + 1))
                    if j >= 1:
                        written(act, ("back", j - 1, 1))
                    nc.scalar.activation(y_t[:], ysum[:], ACT.Copy).then_inc(s_yout, 1)
                elif stage == "turn":
                    q, d, s = a
                    written(act, x_)
                    dst = xn_rev[:, s, PAD:] if d else xn_fwd[:, q, s, PAD:]
                    nc.scalar.activation(dst, scratch(x_), ACT.Identity, scale=col("gamma"),
                                         bias=col("beta")).then_inc(s_read[BANK[x_][0]], 1)
                elif stage == "conv_out":
                    k, h, s = a
                    written(act, x_)
                    if k >= 1:
                        act.wait_ge(s_dtu, 2 * k)
                    nc.scalar.activation(u[:, h, tok(s)], scratch(x_), ACT.Identity,
                                         bias=vec("conv_b", k % 2, h)).then_inc(s_read[BANK[x_][0]], 1)
                elif stage == "z":
                    k, h, s = a
                    written(act, x_)
                    if k >= 1:
                        for t in range(2):
                            was_read(act, ("back", 2 * k - 1, t))
                    nc.scalar.activation(zs[:, h, tok(s)], scratch(x_), ACT.Copy).then_inc(s_read[BANK[x_][0]], 1)
                elif stage == "silu_u":
                    k, = a
                    for h in range(2):
                        for s in range(2):
                            was_read(act, ("conv_out", k, h, s))
                    nc.scalar.activation(u[:], u[:], ACT.Silu).then_inc(s_silu_u, 1)
                elif stage == "silu_z":
                    k, = a
                    for h in range(2):
                        for s in range(2):
                            was_read(act, ("z", k, h, s))
                    nc.scalar.activation(zs[:], zs[:], ACT.Silu).then_inc(s_silu_z, 1)
                elif stage == "xproj":
                    k, s = a
                    written(act, x_)
                    if k >= 1:
                        act.wait_ge(s_cst, 16 * k)
                    else:
                        act.wait_ge(s_ones, 1)
                    nc.scalar.activation(parts[:, k % 2, tok(s)], scratch(x_)[0:ROW_DT, :],
                                         ACT.Copy).then_inc(s_xread, 1)
                    nc.scalar.activation(xdbl[0:32, tok(s)], scratch(x_)[0:32, :], ACT.Copy).then_inc(s_xread, 1)
                    nc.scalar.activation(xdbl[ROW_DT:XROWS, tok(s)], scratch(x_)[ROW_DT:XROWS, :],
                                         ACT.Copy).then_inc(s_xread, 1)
                elif stage == "split":
                    k, = a
                    for s in range(2):
                        was_read(act, ("xproj", k, s))
                    nc.scalar.activation(parts[ROW_MID:ROW_MID + 32, k % 2, :], rest[ROW_MID:ROW_MID + 32, :],
                                         ACT.Copy).then_inc(s_mid, 1)
                    nc.scalar.activation(mid_lo, rest[ROW_LO:ROW_LO + 32, :], ACT.Copy).then_inc(s_mid, 1)
                elif stage == "dt":
                    k, h, s = a
                    written(act, x_)
                    if k >= 1:
                        act.wait_ge(s_dtu, 2 * k)
                    nc.scalar.activation(e[:, h, tok(s)], scratch(x_), ACT.Abs).then_inc(s_own_act, 1)
                    nc.scalar.activation(dt[:, (2 * k + h) % 3, tok(s)], scratch(x_),
                                         ACT.Relu).then_inc(s_read[BANK[x_][0]], 1)
                elif stage == "sp_exp":
                    k, = a
                    act.wait_ge(s_own_act, 4 * (k + 1))
                    nc.scalar.activation(e, e, ACT.Exp, scale=-1.0).then_inc(s_spexp, 1)
                elif stage == "sp_ln":
                    k, h = a
                    act.wait_ge(s_sprest, 2 * k + h + 1)
                    nc.scalar.activation(e[:, h, :], e[:, h, :], ACT.Ln, bias=1.0).then_inc(s_spln, 1)
                elif stage == "skip":
                    k, h = a
                    act.wait_ge(s_silu_u, k + 1)
                    if k >= 1:
                        act.wait_ge(s_seed, 2 * (k - 1) + h + 1)
                    nc.scalar.activation(skip[:, h, :], u[:, h, :], ACT.Copy,
                                         scale=vec("skip", k % 2, h)).then_inc(s_skip, 1)
                elif stage == "ln_apply":
                    w, q = a
                    act.wait_ge(s_shift[w], q + 1)
                    for b in range(BLK):
                        ins = nc.scalar.activation(LN_OUT[w](q)[:, b, :], LN_IN[w](q)[:, b, :], ACT.Identity,
                                                   scale=rstd[:, w, q, b:b + 1], bias=shift[:, w, q, b:b + 1])
                    ins.then_inc(s_norm[w], 1)
                elif stage == "turn_x1":
                    q, s = a
                    written(act, x_)
                    nc.scalar.activation(x1_t[:, tok(s)], scratch(x_), ACT.Copy).then_inc(s_read[BANK[x_][0]], 1)
                elif stage == "ffn_gate":
                    q, s, c = a
                    written(act, x_)
                    nc.scalar.activation(hid[:, c, :], scratch(x_), ACT.Copy).then_inc(s_read[BANK[x_][0]], 1)
                elif stage == "ffn_silu":
                    q, s = a
                    for c in range(3):
                        was_read(act, ("ffn_gate", q, s, c))
                    nc.scalar.activation(hid, hid, ACT.Silu).then_inc(s_hsilu, 1)
                elif stage == "ffn_down":
                    q, s = a
                    written(act, x_)
                    nc.scalar.activation(o[:, s * BPS:(s + 1) * BPS, :],
                                         scratch(x_).rearrange("p (b m) -> p b m", b=BPS),
                                         ACT.Copy).then_inc(s_read[BANK[x_][0]], 1)

        @block.gpsimd
        def _(pool):
            nc.gpsimd.memset(minus_half[:], -0.5).then_inc(s_half, 1)
            nc.gpsimd.memset(da[:, :, :, 0:1], 0.0)
            nc.gpsimd.memset(xn_rev[:, :, 0:PAD], 0.0)
            nc.gpsimd.memset(xn_fwd[:, :, :, 0:PAD], 0.0).then_inc(s_zero, 1)
            pool.wait_ge(s_w, 16)
            nc.gpsimd.tensor_copy(sel[:], col("sel")[0:ROW_DT, :].unsqueeze(2).broadcast_to([ROW_DT, NS, P])
                                  ).then_inc(s_sel, 1)
            pool.wait_ge(s_half, 1)
            for x_ in ORDER:
                stage, a = x_[0], x_[1:]
                if stage == "mul_c":
                    i, = a
                    pool.wait_ge(s_scan, i + 1)
                    if i in c_need:
                        slot, n = c_need[i]
                        pool.wait_ge(s_cl[slot], n)
                    nc.gpsimd.tensor_tensor(hq[:, i % H_RING, :], hq[:, i % H_RING, :],
                                            c_tiles[:, state_of(i) % C_RING, :], ALU.mult).then_inc(s_q, 1)
                elif stage == "ln_pow":
                    w, q = a
                    pool.wait_ge(s_var[w], q + 1)
                    nc.gpsimd.tensor_tensor(rstd[:, w, q, :], rstd[:, w, q, :], minus_half[:],
                                            ALU.pow).then_inc(s_pow[w], 1)

        @block.vector
        def _(dve):
            own = [0]

            def then(ins):
                own[0] += 1
                ins.then_inc(s_own, 1)
                dve.wait_ge(s_own, own[0])

            def setup():
                dve.wait_ge(s_wc, 32)
                for d in range(2):
                    ins = nc.vector.tensor_tensor(wconv[:, d], wconv[:, d],
                                                  w_u_stage[:, d, :].unsqueeze(1).broadcast_to([P, TAPS, DI]),
                                                  ALU.mult)
                ins.then_inc(s_wconv, 1)
                dve.wait_ge(s_expa, 1)
                nc.vector.tensor_scalar(neg_a[:], neg_a[:], -1.0, None, ALU.mult).then_inc(s_nega, 1)
                dve.wait_ge(s_wf, 16)
                nc.vector.tensor_scalar(wffn[:], ffn_stage, 1.0 / 127.0, None, ALU.mult).then_inc(s_wffn, 1)

            nc.vector.memset(xdbl[ROW_DT:P, :], 1.0).then_inc(s_ones, 1)
            for x_ in ORDER:
                stage, a = x_[0], x_[1:]
                if stage == "scan":
                    i, = a
                    j = i // NS
                    if i == 0:
                        dve.wait_ge(s_wffn, 1)
                    dve.wait_ge(s_bcast, i + 1)
                    if i % NS == 0:
                        dve.wait_ge(s_dtu, j + 1)
                    nc.vector.tensor_tensor(bb[:, i % BB_RING, :], bb[:, i % BB_RING, :], dtu[:, j % 3, :],
                                            ALU.mult).then_inc(s_dbu, 1)
                    dve.wait_ge(s_dbu, i + 1)
                    dve.wait_ge(s_exp, i + 1)
                    if i >= H_RING:
                        dve.wait_ge(s_fold, i - H_RING + 1)
                    nc.vector.tensor_tensor_scan(out=hq[:, i % H_RING, :],
                                                 data0=da[:, i % DA_RING].rearrange("p s t -> p (s t)"),
                                                 data1=bb[:, i % BB_RING, :], initial=0.0,
                                                 op0=ALU.mult, op1=ALU.add).then_inc(s_scan, 1)
                elif stage == "ln_stats":
                    w, q = a
                    src = LN_IN[w](q)
                    if w == 0:
                        dve.wait_ge(s_x0, 16 * (q + 1))
                    elif w == 1:
                        dve.wait_ge(s_norm[0], q + 1)
                    elif w == 2:
                        for s in range(2):
                            was_read(dve, ("oproj", q, s))
                    elif w == 3:
                        dve.wait_ge(s_x1, q + 1)
                    else:
                        for s in range(2):
                            was_read(dve, ("ffn_down", q, s))
                    for b in range(BLK):
                        nc.vector.bn_stats(stats[:, w, q, b, :], src[:, b, :]).then_inc(s_stat[w], 1)
                    dve.wait_ge(s_stat[w], BLK * (q + 1) + BLK * q)
                    for b in range(BLK):
                        nc.vector.bn_aggr(mean_var[:, w, q, b, :], stats[:, w, q, b, :]).then_inc(s_stat[w], 1)
                    dve.wait_ge(s_stat[w], 2 * BLK * (q + 1))
                    nc.vector.tensor_scalar(rstd[:, w, q, :], mean_var[:, w, q, :, 1], EPS, None,
                                            ALU.add).then_inc(s_var[w], 1)
                elif stage == "ln_shift":
                    w, q = a
                    dve.wait_ge(s_pow[w], q + 1)
                    nc.vector.scalar_tensor_tensor(out=shift[:, w, q, :], in0=mean_var[:, w, q, :, 0], scalar=-1.0,
                                                   in1=rstd[:, w, q, :], op0=ALU.mult,
                                                   op1=ALU.mult).then_inc(s_shift[w], 1)
                    if w == 1 and q == 0:
                        setup()
                elif stage == "xproj":
                    k, s = a
                    dve.wait_ge(s_xread, 6 * k + 3 * (s + 1))
                    if k >= 1:
                        dve.wait_ge(s_sprest, 2 * k)
                    nc.vector.tensor_tensor(rest[0:ROW_DT, tok(s)], scratch(x_)[0:ROW_DT, :],
                                            parts[:, k % 2, tok(s)], ALU.subtract).then_inc(s_read[BANK[x_][0]], 1)
                elif stage == "split":
                    k, = a
                    dve.wait_ge(s_mid, 2 * (k + 1))
                    rows = slice(ROW_LO, ROW_LO + 32)
                    nc.vector.tensor_tensor(parts[rows, k % 2, :], rest[rows, :], mid_lo,
                                            ALU.subtract).then_inc(s_parts, 1)
                elif stage == "sp_rest":
                    k, h = a
                    g = dt[:, (2 * k + h) % 3, :]
                    if h == 0:
                        dve.wait_ge(s_parts, k + 1)
                        dve.wait_ge(s_spexp, k + 1)
                        for t in range(2):
                            was_read(dve, ("dt", k, 1, t))
                    if k or h:
                        dve.wait_ge(s_sprest, 2 * k + h)
                    then(nc.vector.tensor_scalar(tmp, e[:, h, :], 1.0, -1.0, ALU.add, ALU.add))
                    then(nc.vector.tensor_tensor(tmp, tmp, e[:, h, :], ALU.subtract))
                    nc.vector.tensor_tensor(g, g, tmp, ALU.subtract).then_inc(s_sprest, 1)
                elif stage == "dtu":
                    k, h = a
                    j = 2 * k + h
                    dve.wait_ge(s_spln, j + 1)
                    dve.wait_ge(s_sprest, j + 1)
                    nc.vector.tensor_tensor(dt[:, j % 3, :], dt[:, j % 3, :], e[:, h, :], ALU.add).then_inc(s_dt, 1)
                    dve.wait_ge(s_dt, j + 1)
                    nc.vector.tensor_tensor(dtu[:, j % 3, :], dt[:, j % 3, :], u[:, h, :],
                                            ALU.mult).then_inc(s_dtu, 1)
                elif stage == "back":
                    j, s = a
                    q, d, h = j // 4, j // 2 % 2, j % 2
                    written(dve, x_)
                    dve.wait_ge(s_silu_z, j // 2 + 1)
                    nc.vector.tensor_tensor(gated[:, d, h, tok(s)], scratch(x_), zs[:, h, tok(s)],
                                            ALU.mult).then_inc(s_read[BANK[x_][0]], 1)
                elif stage == "oproj":
                    q, s = a
                    written(dve, x_)
                    if q >= 1:
                        dve.wait_ge(s_out, 16 * q)
                    blk = slice(s * BPS, (s + 1) * BPS)
                    nc.vector.tensor_tensor(o[:, blk, :], scratch(x_).rearrange("p (b m) -> p b m", b=BPS),
                                            attn_in[:, q, blk, :], ALU.add).then_inc(s_read[BANK[x_][0]], 1)
                elif stage == "add_attn":
                    q, = a
                    dve.wait_ge(s_norm[2], q + 1)
                    dve.wait_ge(s_x1in, 16 * (q + 1))
                    nc.vector.tensor_tensor(x1[:], x1[:], normed[:], ALU.add).then_inc(s_x1, 1)
                elif stage == "ffn_up":
                    q, s, c = a
                    if c == 0:
                        dve.wait_ge(s_hsilu, 2 * q + s + 1)
                    written(dve, x_)
                    nc.vector.tensor_tensor(hid[:, c, :], scratch(x_), hid[:, c, :],
                                            ALU.mult).then_inc(s_read[BANK[x_][0]], 1)
                elif stage == "add_ffn":
                    q, = a
                    dve.wait_ge(s_norm[4], q + 1)
                    nc.vector.tensor_tensor(o[:], x1[:], normed[:], ALU.add).then_inc(s_x2, 1)


def kernel(**inputs):
    import numpy as np
    import concourse.bacc as bacc
    from concourse.bass_utils import run_bass_kernel_spmd

    w = {n[len("L0_"):]: np.asarray(a) for n, a in inputs.items()}
    dirs = ("attn_f_", "attn_b_")

    def halves(a):
        return a.reshape((2, P) + a.shape[1:])

    packed = np.zeros((P, NCOLS), np.float32)

    def put(name, a):
        packed[:, COLS[name][0]:COLS[name][1]] = a.reshape(P, -1)

    put("ident", np.eye(P, dtype=np.float32))
    put("rev", np.eye(P, dtype=np.float32)[::-1])
    put("gamma", w["attn_gamma"])
    put("beta", w["attn_beta"])
    for name, key in (("conv_b", "conv_b"), ("skip", "D"), ("a_log", "A_log")):
        put(name, np.stack([np.moveaxis(halves(w[d + key]), 1, 0) for d in dirs], 1))
    sel = np.zeros((P, NS), np.float32)
    for row in (ROW_HI, ROW_LO, ROW_MID):
        sel[row + np.arange(NS), np.arange(NS)] = 1
    put("sel", sel)
    put("wz", np.stack([w[d + "in_w"][DI:].T for d in dirs], 1))
    wx = np.zeros((P, 2, 2, XROWS), np.float32)
    for n, d in enumerate(dirs):
        xp = np.moveaxis(halves(w[d + "xproj_w"].T), 1, 0)
        for row in (ROW_HI, ROW_LO, ROW_MID):
            wx[:, n, :, row:row + NS] = xp[:, :, RANK:RANK + NS]
        wx[:, n, :, NS:2 * NS] = xp[:, :, RANK + NS:]
        wx[:, n, :, ROW_DT:XROWS] = xp[:, :, :RANK]
    put("wx", wx)
    put("wo", np.stack([np.moveaxis(halves(w[d + "out_w"].T), 1, 0) for d in dirs], 1))
    wdt = np.zeros((P, 2, DI), np.float32)
    for n, d in enumerate(dirs):
        wdt[ROW_DT:XROWS, n] = w[d + "dt_w"].T
        wdt[XROWS, n] = w[d + "dt_b"]
    put("wdt", wdt)
    taps = np.stack([np.broadcast_to(w[d + "conv_w"][:, 0, :].T, (P, TAPS, DI)) for d in dirs], 1)
    w_u = np.stack([w[d + "in_w"][:DI].T for d in dirs], 1)
    w_down = np.moveaxis(w["ffn_w_down"].T.reshape(3, P, DM), 1, 0).reshape(P, HID)
    w_ffn = np.concatenate([w["ffn_w_gate"].T, w["ffn_w_up"].T, w_down], 1)

    nc = bacc.Bacc("TRN2", target_bir_lowering=False, num_devices=1)
    arrays = {"x": w["attn_x"], "packed": packed, "conv_taps": taps, "w_u": w_u, "w_ffn": w_ffn}
    arrays = {n + "_dram": np.ascontiguousarray(a) for n, a in arrays.items()}
    args = [nc.dram_tensor(n, a.shape, mybir.dt.from_np(a.dtype), kind="ExternalInput").ap()
            for n, a in arrays.items()]
    args.append(nc.dram_tensor("c_rows_dram", (UNITS, NS, PT), F32, kind="Internal").ap())
    args.append(nc.dram_tensor("out_0_dram", (BATCH, SEQ, DM), F32, kind="ExternalOutput").ap())
    mamba_sandwich(nc, *args)
    r = run_bass_kernel_spmd(nc, [arrays], core_ids=[0])
    return r.results[0]["out_0_dram"]
```

```python
from contextlib import ExitStack

import concourse.bass as bass
from concourse import mybir

P = 128
BATCH, SEQ, DM = 4, 512, 128
DI, NS, RANK, TAPS = 256, 16, 8, 4
HID = 384
PAIRS = 2
PT = BATCH // PAIRS * SEQ
BLK = PT // P
BPS = SEQ // P
UNITS = 2 * PAIRS
SEGS = 2 * UNITS
STEPS = SEGS * NS
EPS = 1e-5

ROW_HI, ROW_LO, ROW_MID, ROW_DT = 0, 32, 64, 96
XROWS = ROW_DT + RANK
COLS = {}
_at = 0
for _name, _n in (("ident", P), ("rev", P), ("gamma", 1), ("beta", 1), ("conv_b", 4), ("skip", 4),
                  ("a_log", 4 * NS), ("sel", NS), ("wz", 2 * DI), ("wx", 4 * XROWS),
                  ("wo", 4 * DM), ("wdt", 2 * DI)):
    COLS[_name] = (_at, _at + _n)
    _at += _n
NCOLS = _at

DA_RING, H_RING, BB_RING, C_RING = 4, 4, 2, 5

ALU = mybir.AluOpType
ACT = mybir.ActivationFunctionType
F32 = mybir.dt.float32
BF16 = mybir.dt.bfloat16
I32 = mybir.dt.int32


def state_of(i):
    k, h, p = i // (2 * NS), i // NS % 2, i % NS
    return p if (k + h) % 2 == 0 else NS - 1 - p


def plan_c_loads():
    keys = [(i // (2 * NS), state_of(i)) for i in range(STEPS)]
    loads, slots, held, last = [], [], [None] * C_RING, [-1] * C_RING

    def next_use(key, i):
        return next((n for n in range(i, STEPS) if keys[n] == key), STEPS)

    for i, key in enumerate(keys):
        if key not in held:
            idle = [n for n in range(C_RING) if held[n] is None or last[n] < i - 2]
            slot = max(idle, key=lambda n: next_use(held[n], i) if held[n] else 2 * STEPS)
            loads.append((*key, slot, i, last[slot]))
            held[slot] = key
        slots.append(held.index(key))
        last[slots[-1]] = i
    return loads, slots


WHOLE, BY_SEQ = ((0, BLK),), ((0, BPS), (BPS, BLK))


def ln_parts(w, q):
    return BY_SEQ if (w < 2 and q == 0) or (w >= 2 and q == PAIRS - 1) else WHOLE


def ln_count(w, q, r):
    return sum(len(ln_parts(w, n)) for n in range(q)) + r + 1


def norm_stages(w, q, r=0):
    lo, hi = ln_parts(w, q)[r]
    stages = [("ln_stats", w, q, b) for b in range(lo // BPS, hi // BPS)] + [("ln_var", w, q, r), ("ln_pow", w, q, r)]
    if len(ln_parts(w, q)) > 1:
        return stages + [("ln_dve", w, q, r)]
    return stages + [("ln_shift", w, q, r)] + [("ln_act", w, q, b) for b in range(lo // BPS, hi // BPS)]


def plan():
    woven = {i: [] for i in range(STEPS + 2)}

    def put(slot, *items):
        woven[slot].extend(items)

    def spread(slots, items):
        for slot, item in zip(slots, items, strict=True):
            put(slot, item)

    def taps(k):
        for h in range(2):
            for s in range(2):
                for t in range(TAPS):
                    yield ("tap", k, h, s, t)

    def half(k, h):
        return [("dt", k, h, 0), ("dt", k, h, 1)] + [(stage, k, h) for stage in (
            "sp_exp", "sp_one", "sp_rest", "sp_ln", "skip", "dt_sub", "dt_add", "dtu")]

    start = []
    for w in range(2):
        parts = [norm_stages(w, 0, r) for r in range(2)]
        start += [x for both in zip(*parts) for x in both]
        start.append(("fold_taps", 0) if w == 0 else ("neg_a",))
    start += [("turn", 0, 0, 0), ("turn", 0, 0, 1)]
    for tap in taps(0):
        start.append(tap)
        if tap[4] == TAPS - 1:
            start.append(("conv_out",) + tap[1:4])
    for s in range(2):
        start += [("xproj_mm", 0, s, 0), ("xproj_mm", 0, s, 1), ("xproj", 0, s), ("xproj_low", 0, s)]
    start += half(0, 0)[:2] + [("split", 0), ("split_low", 0)] + half(0, 0)[2:] + [("exp", 0), ("exp", 1), ("exp", 2), ("bcast", 0), ("bcast", 1)]

    put(0, ("fold_taps", 1), ("turn", 0, 1, 0))
    put(1, ("turn", 0, 1, 1))
    put(20, ("ffn_weights",))
    spread((3, 4, 5, 5, 8, 9, 10), norm_stages(0, 1))
    spread((12, 13, 14, 14, 16, 18, 18), norm_stages(1, 1))
    spread((20, 25, 44, 45), [("turn", 1, d, s) for d in range(2) for s in range(2)])

    for kn, tap_slots, silu in ((1, [*range(1, 17)], 17), (2, [29, 30, 31, *range(34, 47)], 47),
                                (3, [*range(56, 60), *range(62, 69), *range(70, 75)], 75)):
        for slot, tap in zip(tap_slots, taps(kn), strict=True):
            put(slot, tap)
            if tap[4] == TAPS - 1:
                put(slot, ("conv_out",) + tap[1:4])
        put(silu, ("silu_u", kn))
        spread(range(silu + 3, silu + 7), [("xproj_mm", kn, s, h) for s in range(2) for h in range(2)])
        spread((silu + 4, silu + 5, silu + 6, silu + 7),
               [(stage, kn, s) for s in range(2) for stage in ("xproj", "xproj_low")])
        put(silu + 8, ("split", kn))
        put(silu + 9, ("split_low", kn))
        o = silu + 7
        spread((o, o + 1, o + 2, o + 3, o + 4, o + 3, o + 4, o + 5, o + 5, o + 5), half(kn, 0))
    for k, dt_at, z_slots, silu, backs in ((0, 2, (9, 11, 13, 15), 17, (26, 36)), (1, 32, (40, 41, 42, 43), 47, (56, 66)),
                                           (2, 60, (63, 65, 71, 73), 75, (87, 98)), (3, 91, (89, 90, 102, 103), 105, (114, None))):
        o = dt_at
        spread((o, o + 1, o + 3, o + 3, o + 5, o + 4, o + 5, o + 6, o + 7, o + 9), half(k, 1))
        spread(z_slots, [("z", k, h, s) for h in range(2) for s in range(2)])
        put(silu, ("silu_z", k))
        for h in range(2):
            if backs[h] is not None:
                spread(range(backs[h], backs[h] + 4),
                       [(stage, 2 * k + h, s) for s in range(2) for stage in ("back", "gate")])

    spread((75, 76, 77, 78, 81, 84, 85, 86), [("oproj_mm", 0, s, b) for s in range(2) for b in range(BPS)])
    put(79, ("oproj", 0, 0))
    put(86, ("oproj", 0, 1))
    spread((87, 88, 88, 88, 90, 91, 92), norm_stages(2, 0))
    put(94, ("add_attn", 0, 0))
    spread((95, 96, 96, 96, 98, 99, 100), norm_stages(3, 0))
    put(102, ("turn_x1", 0, 0))
    put(103, ("turn_x1", 0, 1))
    spread(range(104, 110), [("ffn_gate", 0, s, c) for s in range(2) for c in range(3)])
    put(110, ("ffn_silu", 0))
    spread((115, 116, 117, 118, 119, 120), [("ffn_up", 0, s, c) for s in range(2) for c in range(3)])
    spread((121, 121, 122, 122, 123, 123, 124, 124), [("ffn_down_mm", 0, s, b) for s in range(2) for b in range(BPS)])
    put(122, ("ffn_down", 0, 0))
    put(124, ("ffn_down", 0, 1))
    spread((125, 126, 126, 126, 129, 129, 129), norm_stages(4, 0))
    put(129, ("add_ffn", 0, 0))

    order = list(start)
    for i in range(STEPS + 2):
        if i < STEPS:
            order += [("scan", i), ("mul_c", i)]
            if i >= 1 and i + 1 < STEPS:
                order.append(("bcast", i + 1))
            if i + DA_RING - 1 < STEPS:
                order.append(("exp", i + DA_RING - 1))
        if i >= 2:
            f = i - 2
            if f % NS == 0:
                order.append(("seed", f // NS))
            order.append(("fold", f))
            if f % NS == NS - 1:
                order += [("y_out", f // NS, s) for s in range(2)]
            if f == STEPS - 1:
                order += [(stage, SEGS - 1, s) for s in range(2) for stage in ("back", "gate")]
        order += woven[i]

    q = PAIRS - 1

    def in_turn(stages):
        return [x for both in zip(stages(0), stages(1)) for x in both]

    for s in range(2):
        order += [("oproj_mm", q, s, b) for b in range(BPS)] + [("oproj", q, s)]
    order += in_turn(lambda r: norm_stages(2, q, r) + [("add_attn", q, r)] + norm_stages(3, q, r))
    order += [("turn_x1", q, s) for s in range(2)]
    for stage in ("ffn_gate", "ffn_up"):
        order += [(stage, q, s, c) for s in range(2) for c in range(3)]
    for s in range(2):
        order += [("ffn_down_mm", q, s, b) for b in range(BPS)] + [("ffn_down", q, s)]
    order += in_turn(lambda r: norm_stages(4, q, r) + [("add_ffn", q, r)])
    return order


PRODUCERS = {"conv_out": "tap", "xproj_low": "xproj_mm", "oproj": "oproj_mm", "ffn_down": "ffn_down_mm", "gate": "back"}
SCRATCH = ("turn", "conv_out", "z", "xproj_low", "dt", "gate", "oproj", "turn_x1", "ffn_gate", "ffn_up", "ffn_down")


def plan_banks(order):
    readers = {m: stage for stage, m in PRODUCERS.items()}
    first, last = {}, {}
    for n, x in enumerate(order):
        key = (readers[x[0]],) + x[1:4 if x[0] == "tap" else 3] if x[0] in readers else x
        if key[0] in SCRATCH:
            first.setdefault(key, n)
            last[key] = n
    banks, uses, busy = {}, [0, 0], [-1, -1]
    for key in sorted(first, key=first.get):
        bank = busy.index(min(busy))
        assert busy[bank] < first[key], (key, order[first[key]-5:first[key]+5], busy, first[key], last[key])
        busy[bank] = last[key]
        uses[bank] += 1
        banks[key] = (bank, uses[bank])
    return banks


def mamba_sandwich(nc, x, packed, conv_taps, w_u, w_ffn, c_rows, out):
    ORDER = plan()
    BANK = plan_banks(ORDER)
    C_LOADS, C_SLOT = plan_c_loads()
    c_need, c_count = {}, [0] * C_RING
    for k, n, slot, step, _ in C_LOADS:
        c_count[slot] += 1
        c_need[step] = (slot, 16 * c_count[slot])

    with ExitStack() as ctx:
        def sb(name, shape, dt=F32):
            return ctx.enter_context(nc.sbuf_tensor(name, shape, dt))

        def sem(name):
            return ctx.enter_context(nc.semaphore(name))

        bb = ctx.enter_context(nc.psum_tensor("bb", [P, BB_RING, PT], F32))
        ysum = ctx.enter_context(nc.psum_tensor("ysum", [P, PT], F32))
        scr = ctx.enter_context(nc.psum_tensor("scr", [P, 2, SEQ], F32))

        wts = sb("wts", [P, NCOLS])
        wconv = sb("wconv", [P, 2, TAPS, DI])
        neg_a = sb("neg_a", [P, 4 * NS])
        sel = sb("sel", [ROW_DT, NS, P], BF16)
        wffn = sb("wffn", [P, 3 * HID])
        stats = sb("stats", [P, 5, PAIRS, BLK, 6])
        mean_var = sb("mean_var", [P, 5, PAIRS, BLK, 2])
        rstd = sb("rstd", [P, 5, PAIRS, BLK])
        shift = sb("shift", [P, 5, PAIRS, BLK])
        minus_half = sb("minus_half", [P, BLK])
        x0 = sb("x0", [P, BLK, DM])
        attn_in = sb("attn_in", [P, PAIRS, BLK, DM])
        normed = sb("normed", [P, BLK, DM])
        x1 = sb("x1", [P, BLK, DM])
        o = sb("o", [P, BLK, DM])
        PAD = TAPS - 1
        xn_fwd = sb("xn_fwd", [P, PAIRS, 2, PAD + SEQ])
        xn_rev = sb("xn_rev", [P, 2, PAD + SEQ])
        u = sb("u", [P, 2, PT])
        zs = sb("zs", [P, 2, PT])
        skip = sb("skip", [P, 2, PT])
        parts = sb("parts", [ROW_DT, 2, PT], BF16)
        xdbl = sb("xdbl", [P, PT])
        dt = sb("dt", [P, 3, PT])
        dtu = sb("dtu", [P, 3, PT])
        work = sb("work", [P, 3 * PT])
        da = sb("da", [P, DA_RING, 2, SEQ])
        hq = sb("hq", [P, H_RING, PT])
        c_tiles = sb("c_tiles", [P, C_RING, PT])
        y_t = sb("y_t", [P, PT])
        gated = sb("gated", [P, 2, 2, PT])

        e = work[:, 0:PT]
        ln_one = work[:, PT:2 * PT]
        tmp = work[:, 2 * PT:3 * PT]
        x1_t = work[:, 0:PT]
        hid_first = [work[:, PT + c * SEQ:PT + (c + 1) * SEQ] for c in range(3)]
        rest = tmp
        mid_lo = xdbl[ROW_LO:ROW_LO + 32, 0:PT // 2].bitcast(BF16)
        w_u_stage = gated[:, 0, 0, 0:2 * DI].rearrange("p (d e) -> p d e", d=2)
        ffn_stage = gated[:, 1].rearrange("p h t -> p (h t)")[:, 0:3 * HID].bitcast(I32)
        hid_second = [xn_rev[:, 0, 0:SEQ], xn_rev[:, 1, 0:SEQ], xn_fwd[:, 0, 0, 0:SEQ]]
        out_end = x0

        def col(name):
            return wts[:, COLS[name][0]:COLS[name][1]]

        ident, rev = col("ident"), col("rev")
        wz = col("wz").rearrange("p (d e) -> p d e", d=2)
        wx = col("wx").rearrange("p (d h r) -> p d h r", d=2, h=2)
        wo = col("wo").rearrange("p (d h m) -> p d h m", d=2, h=2)
        wdt = col("wdt").rearrange("p (d e) -> p d e", d=2)
        perm = [ident, rev]
        w_gate, w_up, w_down = (wffn[:, n * HID:(n + 1) * HID] for n in range(3))

        def vec(name, d, h):
            c = COLS[name][0] + 2 * d + h
            return wts[:, c:c + 1]

        s_x0 = [sem("x0_first_loaded"), sem("x0_second_loaded")]
        s_x1in = sem("x1_holds_x0")
        s_w = sem("packed_loaded")
        s_wc = [sem("fwd_taps_loaded"), sem("rev_taps_loaded")]
        s_wf = sem("ffn_weights_loaded")
        s_zero = sem("zeros_set")
        s_wconv = sem("conv_folded")
        s_wffn = sem("ffn_dequantised")
        s_expa = sem("exp_a_log_done")
        s_nega = sem("neg_a_done")
        s_sel = sem("selector_done")
        s_full = [sem("scratch0_written"), sem("scratch1_written")]
        s_read = [sem("scratch0_read"), sem("scratch1_read")]
        s_bcast = sem("b_broadcast")
        s_dbu = sem("dbu_done")
        s_exp = sem("da_done")
        s_scan = sem("scan_done")
        s_q = sem("c_product_done")
        s_fold = sem("state_summed")
        s_seed = sem("skip_seeded")
        s_yout = sem("y_copied")
        s_cl = [sem(f"c_tile{n}_loaded") for n in range(C_RING)]
        s_cst = sem("c_rows_stored")
        s_xread = sem("xdbl_rows_copied")
        s_mid = sem("middle_parts_done")
        s_parts = sem("b_parts_done")
        s_silu_u = sem("u_silu_done")
        s_silu_z = sem("z_silu_done")
        s_spexp = sem("softplus_exp_done")
        s_sprest = sem("softplus_rest_done")
        s_sub = sem("softplus_rest_taken_off")
        s_spln = sem("softplus_ln_done")
        s_dt = sem("dt_done")
        s_dtu = sem("dtu_done")
        s_skip = sem("skip_done")
        s_stat = [sem(f"ln{w}_stats_done") for w in range(5)]
        s_var = [sem(f"ln{w}_var_done") for w in range(5)]
        s_pow = [sem(f"ln{w}_rstd_done") for w in range(5)]
        s_shift = [sem(f"ln{w}_shift_done") for w in range(5)]
        s_norm = [sem(f"ln{w}_applied") for w in range(5)]
        s_x1 = sem("x1_done")
        s_hsilu = sem("gate_silu_done")
        s_x2 = sem("x2_done")
        s_out = sem("out_stored")
        s_one = sem("one_plus_e_done")
        s_own = sem("dve_own_step")
        s_abs = sem("softplus_abs_done")
        s_ones = sem("ones_row_set")
        s_half = sem("minus_half_set")

        x_tok = x.rearrange("s (b p) m -> p s b m", p=P)
        out_tok = out.rearrange("s (b p) m -> p s b m", p=P)

        def pair_of(ap, q):
            return ap[:, 2 * q:2 * q + 2, :, :]

        def by_seq(tile):
            return tile.rearrange("p (s b) m -> p s b m", s=2)

        def scratch(stage):
            return scr[:, BANK[stage][0], :]

        def may_write(eng, stage):
            b, n = BANK[stage]
            if n > 1:
                eng.wait_ge(s_read[b], n - 1)

        def written(eng, stage):
            b, n = BANK[stage]
            eng.wait_ge(s_full[b], n)

        def was_read(eng, stage):
            b, n = BANK[stage]
            eng.wait_ge(s_read[b], n)

        def tok(s):
            return slice(s * SEQ, (s + 1) * SEQ)

        def u_ready(eng, k):
            if k == 0:
                for h in range(2):
                    for s in range(2):
                        was_read(eng, ("conv_out", 0, h, s))
            else:
                eng.wait_ge(s_silu_u, k)

        def soft_plus(engine, wait_on, stage, k, h):
            j = 2 * k + h
            g = dt[:, j % 3, :]
            if stage == "dt_sub":
                wait_on.wait_ge(s_sprest, j + 1)
                was_read(wait_on, ("dt", k, h, 1))
                engine.tensor_tensor(g, g, tmp, ALU.subtract).then_inc(s_sub, 1)
            else:
                wait_on.wait_ge(s_spln, j + 1)
                wait_on.wait_ge(s_sub, j + 1)
                engine.tensor_tensor(g, g, ln_one, ALU.add).then_inc(s_dt, 1)

        def blocks(s):
            return slice(s * BPS, (s + 1) * BPS)

        def hid(s, c):
            return (hid_first, hid_second)[s][c]

        LN_IN = [lambda q: x0, lambda q: attn_in[:, q], lambda q: o, lambda q: x1, lambda q: o]
        LN_OUT = [lambda q: attn_in[:, q], lambda q: normed, lambda q: normed, lambda q: normed,
                  lambda q: normed]

        block = ctx.enter_context(nc.Block())

        @block.sync
        def _(sp):
            for s in range(2):
                sp.dma_start(x0[:, s * BPS:(s + 1) * BPS, :], x_tok[:, s]).then_inc(s_x0[s], 16)
            sp.dma_start(wts[:], packed).then_inc(s_w, 16)
            for d in range(2):
                sp.dma_start(w_u_stage[:, d], w_u[:, d]).then_inc(s_wc[d], 16)
                sp.dma_start(wconv[:, d], conv_taps[:, d]).then_inc(s_wc[d], 16)
            sp.dma_start(ffn_stage, w_ffn).then_inc(s_wf, 16)
            sp.dma_start(by_seq(x1[:]), pair_of(x_tok, 0)).then_inc(s_x1in, 16)
            sp.wait_ge(s_norm[0], ln_count(0, 0, 1))
            for s in range(2):
                sp.dma_start(x0[:, s * BPS:(s + 1) * BPS, :], x_tok[:, 2 + s]).then_inc(s_x0[s], 16)
            stored = -1
            for k, n, slot, step, free in C_LOADS:
                if k > stored:
                    sp.wait_ge(s_xread, 6 * (k + 1))
                    sp.dma_start(c_rows[k], xdbl[NS:2 * NS, :]).then_inc(s_cst, 16)
                    sp.wait_ge(s_cst, 16 * (k + 1))
                    stored = k
                if free >= 0:
                    sp.wait_ge(s_q, free + 1)
                sp.dma_start(c_tiles[:, slot, :], c_rows[k, n].partition_broadcast(P)).then_inc(s_cl[slot], 16)
            sp.wait_ge(s_x2, 1)
            sp.dma_start(pair_of(out_tok, 0), by_seq(o[:])).then_inc(s_out, 16)
            sp.dma_start(by_seq(x1[:]), pair_of(x_tok, 1)).then_inc(s_x1in, 16)
            for s in range(2):
                sp.wait_ge(s_x2, 2 + s)
                sp.dma_start(out_tok[:, 2 + s], out_end[:, s * BPS:(s + 1) * BPS, :]).then_inc(s_out, 16)
            sp.wait_ge(s_out, 48)

        @block.tensor
        def _(pe):
            pe.wait_ge(s_w, 16)
            for x_ in ORDER:
                stage, a = x_[0], x_[1:]
                if stage == "bcast":
                    i, = a
                    k = i // (2 * NS)
                    if i == 0:
                        pe.wait_ge(s_sel, 1)
                    if i % (2 * NS) == 0:
                        pe.wait_ge(s_parts, k + 1)
                    if i >= BB_RING:
                        pe.wait_ge(s_scan, i - BB_RING + 1)
                    n = state_of(i)
                    for s in range(2):
                        mm = nc.tensor.matmul(bb[:, i % BB_RING, tok(s)], sel[:, n, :], parts[:, k % 2, tok(s)],
                                              start=True, stop=True)
                    mm.then_inc(s_bcast, 1)
                elif stage == "seed":
                    j, = a
                    pe.wait_ge(s_skip, j + 1)
                    if j >= 1:
                        pe.wait_ge(s_yout, 2 * j)
                    for b in range(BLK):
                        mm = nc.tensor.matmul(ysum[:, b * P:(b + 1) * P], skip[:, j % 2, b * P:(b + 1) * P],
                                              ident, start=(b % BPS == 0), stop=False, is_transpose=True,
                                              skip_group_check=True)
                    mm.then_inc(s_seed, 1)
                elif stage == "fold":
                    i, = a
                    pe.wait_ge(s_q, i + 1)
                    for b in range(BLK):
                        mm = nc.tensor.matmul(ysum[:, b * P:(b + 1) * P], hq[:, i % H_RING, b * P:(b + 1) * P],
                                              ident, start=False, stop=(i % NS == NS - 1), is_transpose=True,
                                              skip_group_check=True)
                    mm.then_inc(s_fold, 1)
                elif stage == "back":
                    j, s = a
                    use = ("gate", j, s)
                    pe.wait_ge(s_yout, 2 * j + s + 1)
                    may_write(pe, use)
                    d = j // 2 % 2
                    for b in range(BPS):
                        src = s * BPS + (BPS - 1 - b if d else b)
                        mm = nc.tensor.matmul(scratch(use)[:, b * P:(b + 1) * P], y_t[:, src * P:(src + 1) * P],
                                              perm[d], start=True, stop=True, is_transpose=True)
                    mm.then_inc(s_full[BANK[use][0]], 1)
                elif stage == "turn":
                    q, d, s = a
                    pe.wait_ge(s_norm[1], 2 * q + s + 1)
                    may_write(pe, x_)
                    for b in range(BPS):
                        src = s * BPS + (BPS - 1 - b if d else b)
                        mm = nc.tensor.matmul(scratch(x_)[:, b * P:(b + 1) * P], normed[:, src, :],
                                              perm[d], start=True, stop=True, is_transpose=True)
                    mm.then_inc(s_full[BANK[x_][0]], 1)
                elif stage == "tap":
                    k, h, s, t = a
                    q, d = k // 2, k % 2
                    use = ("conv_out", k, h, s)
                    if t == 0:
                        pe.wait_ge(s_wconv, d + 1)
                        pe.wait_ge(s_zero, 1)
                        was_read(pe, ("turn", q, d, s))
                        may_write(pe, use)
                    src = xn_rev[:, s, t:t + SEQ] if d else xn_fwd[:, q, s, t:t + SEQ]
                    mm = nc.tensor.matmul(scratch(use), wconv[:, d, t, h * P:(h + 1) * P], src,
                                          start=(t == 0), stop=(t == TAPS - 1))
                    if t == TAPS - 1:
                        mm.then_inc(s_full[BANK[use][0]], 1)
                elif stage == "z":
                    k, h, s = a
                    q, d = k // 2, k % 2
                    was_read(pe, ("turn", q, 0, s))
                    may_write(pe, x_)
                    nc.tensor.matmul(scratch(x_), wz[:, d, h * P:(h + 1) * P], xn_fwd[:, q, s, PAD:PAD + SEQ],
                                     start=True, stop=True).then_inc(s_full[BANK[x_][0]], 1)
                elif stage == "xproj_mm":
                    k, s, h = a
                    use = ("xproj_low", k, s)
                    if h == 0:
                        u_ready(pe, k)
                        may_write(pe, use)
                    mm = nc.tensor.matmul(scratch(use)[0:XROWS, :], wx[:, k % 2, h, :], u[:, h, tok(s)],
                                          start=(h == 0), stop=(h == 1))
                    if h == 1:
                        mm.then_inc(s_full[BANK[use][0]], 1)
                elif stage == "dt":
                    k, h, s = a
                    pe.wait_ge(s_xread, 6 * (k + 1))
                    pe.wait_ge(s_ones, 1)
                    may_write(pe, x_)
                    rows = slice(ROW_DT, XROWS + 1)
                    nc.tensor.matmul(scratch(x_), wdt[rows, k % 2, h * P:(h + 1) * P], xdbl[rows, tok(s)],
                                     start=True, stop=True).then_inc(s_full[BANK[x_][0]], 1)
                elif stage == "oproj_mm":
                    q, s, b = a
                    use = ("oproj", q, s)
                    if b == 0:
                        was_read(pe, ("gate", 4 * q + 3, s))
                        may_write(pe, use)
                    at = slice((s * BPS + b) * P, (s * BPS + b + 1) * P)
                    for n in range(4):
                        mm = nc.tensor.matmul(scratch(use)[:, b * P:(b + 1) * P], gated[:, n // 2, n % 2, at],
                                              wo[:, n // 2, n % 2, :], start=(b == 0 and n == 0), stop=(n == 3),
                                              skip_group_check=True)
                    if b == BPS - 1:
                        mm.then_inc(s_full[BANK[use][0]], 1)
                elif stage == "turn_x1":
                    q, s = a
                    pe.wait_ge(s_norm[3], 2 * q + s + 1)
                    may_write(pe, x_)
                    for b in range(BPS):
                        mm = nc.tensor.matmul(scratch(x_)[:, b * P:(b + 1) * P], normed[:, s * BPS + b, :],
                                              ident, start=True, stop=True, is_transpose=True)
                    mm.then_inc(s_full[BANK[x_][0]], 1)
                elif stage in ("ffn_gate", "ffn_up"):
                    q, s, c = a
                    if c == 0 and stage == "ffn_gate":
                        pe.wait_ge(s_wffn, 1)
                        was_read(pe, ("turn_x1", q, s))
                    may_write(pe, x_)
                    w = w_gate if stage == "ffn_gate" else w_up
                    nc.tensor.matmul(scratch(x_), w[:, c * P:(c + 1) * P], x1_t[:, tok(s)],
                                     start=True, stop=True).then_inc(s_full[BANK[x_][0]], 1)
                elif stage == "ffn_down_mm":
                    q, s, b = a
                    use = ("ffn_down", q, s)
                    if b == 0:
                        for c in range(3):
                            was_read(pe, ("ffn_up", q, s, c))
                        may_write(pe, use)
                    for c in range(3):
                        mm = nc.tensor.matmul(scratch(use)[:, b * P:(b + 1) * P],
                                              hid(s, c)[:, b * P:(b + 1) * P],
                                              w_down[:, c * P:(c + 1) * P], start=(b == 0 and c == 0),
                                              stop=(c == 2), skip_group_check=True)
                    if b == BPS - 1:
                        mm.then_inc(s_full[BANK[use][0]], 1)

        @block.scalar
        def _(act):
            act.wait_ge(s_w, 16)
            nc.scalar.activation(neg_a[:], col("a_log"), ACT.Exp).then_inc(s_expa, 1)
            nc.scalar.activation(sel[:], col("sel")[0:ROW_DT, :].unsqueeze(2).broadcast_to([ROW_DT, NS, P]),
                                 ACT.Copy).then_inc(s_sel, 1)
            for x_ in ORDER:
                stage, a = x_[0], x_[1:]
                if stage == "exp":
                    i, = a
                    j = i // NS
                    if i == 0:
                        act.wait_ge(s_nega, 1)
                        act.wait_ge(s_zero, 1)
                    if i % NS == 0:
                        act.wait_ge(s_dt, j + 1)
                    if i >= DA_RING:
                        act.wait_ge(s_scan, i - DA_RING + 1)
                    c = (j % 4) * NS + state_of(i)
                    nc.scalar.activation(da[:, i % DA_RING, :, 1:SEQ],
                                         dt[:, j % 3, :].rearrange("p (s t) -> p s t", s=2)[:, :, 1:SEQ],
                                         ACT.Exp, scale=neg_a[:, c:c + 1]).then_inc(s_exp, 1)
                elif stage == "y_out":
                    j, s = a
                    act.wait_ge(s_fold, NS * (j + 1))
                    if j >= 1:
                        written(act, ("gate", j - 1, s))
                    nc.scalar.activation(y_t[:, tok(s)], ysum[:, tok(s)], ACT.Copy).then_inc(s_yout, 1)
                elif stage == "turn":
                    q, d, s = a
                    written(act, x_)
                    dst = xn_rev[:, s, PAD:] if d else xn_fwd[:, q, s, PAD:]
                    nc.scalar.activation(dst, scratch(x_), ACT.Identity, scale=col("gamma"),
                                         bias=col("beta")).then_inc(s_read[BANK[x_][0]], 1)
                elif stage == "conv_out":
                    k, h, s = a
                    written(act, x_)
                    if k >= 1:
                        act.wait_ge(s_dtu, 2 * (k - 1) + h + 1)
                        act.wait_ge(s_skip, 2 * (k - 1) + h + 1)
                    nc.scalar.activation(u[:, h, tok(s)], scratch(x_), ACT.Silu if k == 0 else ACT.Identity,
                                         bias=vec("conv_b", k % 2, h)).then_inc(s_read[BANK[x_][0]], 1)
                elif stage == "z":
                    k, h, s = a
                    written(act, x_)
                    if k >= 1:
                        for t in range(2):
                            was_read(act, ("gate", 2 * (k - 1) + h, t))
                    nc.scalar.activation(zs[:, h, tok(s)], scratch(x_), ACT.Copy).then_inc(s_read[BANK[x_][0]], 1)
                elif stage == "silu_u":
                    k, = a
                    for h in range(2):
                        for s in range(2):
                            was_read(act, ("conv_out", k, h, s))
                    nc.scalar.activation(u[:], u[:], ACT.Silu).then_inc(s_silu_u, 1)
                elif stage == "silu_z":
                    k, = a
                    for h in range(2):
                        for s in range(2):
                            was_read(act, ("z", k, h, s))
                    nc.scalar.activation(zs[:], zs[:], ACT.Silu).then_inc(s_silu_z, 1)
                elif stage == "xproj":
                    k, s = a
                    use = ("xproj_low", k, s)
                    written(act, use)
                    if k >= 1:
                        act.wait_ge(s_cst, 16 * k)
                    else:
                        act.wait_ge(s_ones, 1)
                    nc.scalar.activation(parts[:, k % 2, tok(s)], scratch(use)[0:ROW_DT, :],
                                         ACT.Copy).then_inc(s_xread, 1)
                    nc.scalar.activation(xdbl[ROW_DT:XROWS, tok(s)], scratch(use)[ROW_DT:XROWS, :],
                                         ACT.Copy).then_inc(s_xread, 1)
                    nc.scalar.activation(xdbl[0:32, tok(s)], scratch(use)[0:32, :], ACT.Copy).then_inc(s_xread, 1)
                elif stage == "split":
                    k, = a
                    for s in range(2):
                        was_read(act, ("xproj_low", k, s))
                    nc.scalar.activation(mid_lo, rest[ROW_LO:ROW_LO + 32, :], ACT.Copy).then_inc(s_mid, 1)
                    nc.scalar.activation(parts[ROW_MID:ROW_MID + 32, k % 2, :], rest[ROW_MID:ROW_MID + 32, :],
                                         ACT.Copy).then_inc(s_mid, 1)
                elif stage == "dt":
                    k, h, s = a
                    written(act, x_)
                    j = 2 * k + h
                    if j >= 1:
                        act.wait_ge(s_sprest, j)
                        act.wait_ge(s_spln, j)
                    if j >= 3:
                        act.wait_ge(s_dtu, j - 2)
                    nc.scalar.activation(e[:, tok(s)], scratch(x_), ACT.Abs).then_inc(s_abs, 1)
                    nc.scalar.activation(dt[:, (2 * k + h) % 3, tok(s)], scratch(x_),
                                         ACT.Relu).then_inc(s_read[BANK[x_][0]], 1)
                elif stage == "sp_exp":
                    k, h = a
                    act.wait_ge(s_abs, 4 * k + 2 * h + 2)
                    nc.scalar.activation(e, e, ACT.Exp, scale=-1.0).then_inc(s_spexp, 1)
                elif stage == "sp_one":
                    k, h = a
                    act.wait_ge(s_spexp, 2 * k + h + 1)
                    act.wait_ge(s_parts, k + 1)
                    if k or h:
                        act.wait_ge(s_sub, 2 * k + h)
                    nc.scalar.activation(tmp, e, ACT.Identity, bias=1.0).then_inc(s_one, 1)
                elif stage == "sp_ln":
                    k, h = a
                    if k or h:
                        act.wait_ge(s_dt, 2 * k + h)
                    nc.scalar.activation(ln_one, e, ACT.Ln, bias=1.0).then_inc(s_spln, 1)
                elif stage == "skip":
                    k, h = a
                    u_ready(act, k)
                    if k >= 1:
                        act.wait_ge(s_seed, 2 * (k - 1) + h + 1)
                    nc.scalar.activation(skip[:, h, :], u[:, h, :], ACT.Copy,
                                         scale=vec("skip", k % 2, h)).then_inc(s_skip, 1)
                elif stage == "ln_act":
                    w, q, s = a
                    act.wait_ge(s_shift[w], 1)
                    for b in range(s * BPS, (s + 1) * BPS):
                        ins = nc.scalar.activation(LN_OUT[w](q)[:, b, :], LN_IN[w](q)[:, b, :], ACT.Identity,
                                                   scale=rstd[:, w, q, b:b + 1], bias=shift[:, w, q, b:b + 1])
                    ins.then_inc(s_norm[w], 1)
                elif stage == "turn_x1":
                    q, s = a
                    written(act, x_)
                    act.wait_ge(s_dt, SEGS)
                    nc.scalar.activation(x1_t[:, tok(s)], scratch(x_), ACT.Copy).then_inc(s_read[BANK[x_][0]], 1)
                elif stage == "ffn_gate":
                    q, s, c = a
                    written(act, x_)
                    nc.scalar.activation(hid(s, c), scratch(x_), ACT.Copy if q == 0 else ACT.Silu
                                         ).then_inc(s_read[BANK[x_][0]], 1)
                elif stage == "ffn_silu":
                    q, = a
                    for s in range(2):
                        for c in range(3):
                            was_read(act, ("ffn_gate", q, s, c))
                            nc.scalar.activation(hid(s, c), hid(s, c), ACT.Silu).then_inc(s_hsilu, 1)
                elif stage == "ffn_down":
                    q, s = a
                    written(act, x_)
                    nc.scalar.activation(o[:, blocks(s), :], scratch(x_).rearrange("p (b m) -> p b m", b=BPS),
                                         ACT.Copy).then_inc(s_read[BANK[x_][0]], 1)

        @block.gpsimd
        def _(pool):
            nc.gpsimd.memset(minus_half[:], -0.5).then_inc(s_half, 1)
            nc.gpsimd.memset(da[:, :, :, 0:1], 0.0)
            nc.gpsimd.memset(xn_rev[:, :, 0:PAD], 0.0)
            nc.gpsimd.memset(xn_fwd[:, :, :, 0:PAD], 0.0).then_inc(s_zero, 1)
            pool.wait_ge(s_half, 1)
            for x_ in ORDER:
                stage, a = x_[0], x_[1:]
                if stage == "mul_c":
                    i, = a
                    pool.wait_ge(s_scan, i + 1)
                    if i in c_need:
                        slot, n = c_need[i]
                        pool.wait_ge(s_cl[slot], n)
                    nc.gpsimd.tensor_tensor(hq[:, i % H_RING, :], hq[:, i % H_RING, :],
                                            c_tiles[:, C_SLOT[i], :], ALU.mult).then_inc(s_q, 1)
                elif stage in ("dt_sub", "dt_add") and a[1] == 1:
                    soft_plus(nc.gpsimd, pool, stage, *a)
                elif stage == "ln_pow":
                    w, q, r = a
                    pool.wait_ge(s_var[w], ln_count(w, q, r))
                    at = slice(*ln_parts(w, q)[r])
                    nc.gpsimd.tensor_tensor(rstd[:, w, q, at], rstd[:, w, q, at], minus_half[:, at],
                                            ALU.pow).then_inc(s_pow[w], 1)

        @block.vector
        def _(dve):
            own = [0]

            def then(ins):
                own[0] += 1
                ins.then_inc(s_own, 1)
                dve.wait_ge(s_own, own[0])

            nc.vector.memset(xdbl[ROW_DT:P, :], 1.0).then_inc(s_ones, 1)
            for x_ in ORDER:
                stage, a = x_[0], x_[1:]
                if stage == "scan":
                    i, = a
                    j = i // NS
                    dve.wait_ge(s_bcast, i + 1)
                    if i % NS == 0:
                        dve.wait_ge(s_dtu, j + 1)
                    nc.vector.tensor_tensor(bb[:, i % BB_RING, :], bb[:, i % BB_RING, :], dtu[:, j % 3, :],
                                            ALU.mult).then_inc(s_dbu, 1)
                    dve.wait_ge(s_dbu, i + 1)
                    dve.wait_ge(s_exp, i + 1)
                    if i >= H_RING:
                        dve.wait_ge(s_fold, i - H_RING + 1)
                    nc.vector.tensor_tensor_scan(out=hq[:, i % H_RING, :],
                                                 data0=da[:, i % DA_RING].rearrange("p s t -> p (s t)"),
                                                 data1=bb[:, i % BB_RING, :], initial=0.0,
                                                 op0=ALU.mult, op1=ALU.add).then_inc(s_scan, 1)
                elif stage == "ln_stats":
                    w, q, s = a
                    src = LN_IN[w](q)
                    if w == 0:
                        dve.wait_ge(s_x0[s], 16 * (q + 1))
                    elif w == 1:
                        dve.wait_ge(s_norm[0], 2 * q + s + 1)
                    elif w == 2:
                        was_read(dve, ("oproj", q, s))
                    elif w == 3:
                        dve.wait_ge(s_x1, q + 1 if q == 0 else q + 1 + s)
                    else:
                        was_read(dve, ("ffn_down", q, s))
                    for b in range(s * BPS, (s + 1) * BPS):
                        nc.vector.bn_stats(stats[:, w, q, b, :], src[:, b, :]).then_inc(s_stat[w], 1)
                    done = 2 * BPS * (2 * q + s)
                    dve.wait_ge(s_stat[w], done + BPS)
                    for b in range(s * BPS, (s + 1) * BPS):
                        nc.vector.bn_aggr(mean_var[:, w, q, b, :], stats[:, w, q, b, :]).then_inc(s_stat[w], 1)
                elif stage == "ln_var":
                    w, q, r = a
                    lo, hi = ln_parts(w, q)[r]
                    dve.wait_ge(s_stat[w], 2 * (BLK * q + hi))
                    nc.vector.tensor_scalar(rstd[:, w, q, lo:hi], mean_var[:, w, q, lo:hi, 1], EPS, None,
                                            ALU.add).then_inc(s_var[w], 1)
                elif stage == "ln_shift":
                    w, q, r = a
                    dve.wait_ge(s_pow[w], ln_count(w, q, r))
                    nc.vector.scalar_tensor_tensor(out=shift[:, w, q, :], in0=mean_var[:, w, q, :, 0], scalar=-1.0,
                                                   in1=rstd[:, w, q, :], op0=ALU.mult,
                                                   op1=ALU.mult).then_inc(s_shift[w], 1)
                elif stage == "ln_dve":
                    w, q, r = a
                    dve.wait_ge(s_pow[w], ln_count(w, q, r))
                    for b in range(*ln_parts(w, q)[r]):
                        ins = nc.vector.tensor_scalar(LN_OUT[w](q)[:, b, :], LN_IN[w](q)[:, b, :],
                                                      mean_var[:, w, q, b, 0:1], rstd[:, w, q, b:b + 1],
                                                      ALU.subtract, ALU.mult)
                    ins.then_inc(s_norm[w], 1)
                elif stage == "fold_taps":
                    d, = a
                    dve.wait_ge(s_wc[d], 32)
                    nc.vector.tensor_tensor(wconv[:, d], wconv[:, d],
                                            w_u_stage[:, d, :].unsqueeze(1).broadcast_to([P, TAPS, DI]),
                                            ALU.mult).then_inc(s_wconv, 1)
                elif stage == "neg_a":
                    dve.wait_ge(s_expa, 1)
                    nc.vector.tensor_scalar(neg_a[:], neg_a[:], -1.0, None, ALU.mult).then_inc(s_nega, 1)
                elif stage == "ffn_weights":
                    dve.wait_ge(s_wf, 16)
                    nc.vector.tensor_scalar(wffn[:], ffn_stage, 1.0 / 127.0, None, ALU.mult).then_inc(s_wffn, 1)
                elif stage == "xproj_low":
                    k, s = a
                    dve.wait_ge(s_xread, 6 * k + 3 * (s + 1))
                    if k >= 1:
                        dve.wait_ge(s_sub, 2 * k)
                    nc.vector.tensor_tensor(rest[0:ROW_DT, tok(s)], scratch(x_)[0:ROW_DT, :],
                                            parts[:, k % 2, tok(s)], ALU.subtract).then_inc(s_read[BANK[x_][0]], 1)
                elif stage == "split_low":
                    k, = a
                    dve.wait_ge(s_mid, 2 * (k + 1))
                    rows = slice(ROW_LO, ROW_LO + 32)
                    nc.vector.tensor_tensor(parts[rows, k % 2, :], rest[rows, :], mid_lo,
                                            ALU.subtract).then_inc(s_parts, 1)
                elif stage == "sp_rest":
                    k, h = a
                    dve.wait_ge(s_one, 2 * k + h + 1)
                    nc.vector.scalar_tensor_tensor(out=tmp, in0=tmp, scalar=-1.0, in1=e, op0=ALU.add,
                                                   op1=ALU.subtract).then_inc(s_sprest, 1)
                elif stage in ("dt_sub", "dt_add") and a[1] == 0:
                    soft_plus(nc.vector, dve, stage, *a)
                elif stage == "dtu":
                    k, h = a
                    j = 2 * k + h
                    dve.wait_ge(s_dt, j + 1)
                    u_ready(dve, k)
                    nc.vector.tensor_tensor(dtu[:, j % 3, :], dt[:, j % 3, :], u[:, h, :],
                                            ALU.mult).then_inc(s_dtu, 1)
                elif stage == "gate":
                    j, s = a
                    q, d, h = j // 4, j // 2 % 2, j % 2
                    written(dve, x_)
                    dve.wait_ge(s_silu_z, j // 2 + 1)
                    if q >= 1:
                        was_read(dve, ("oproj", q - 1, s))
                    nc.vector.tensor_tensor(gated[:, d, h, tok(s)], scratch(x_), zs[:, h, tok(s)],
                                            ALU.mult).then_inc(s_read[BANK[x_][0]], 1)
                elif stage == "oproj":
                    q, s = a
                    written(dve, x_)
                    if q >= 1:
                        dve.wait_ge(s_out, 16 * q)
                    nc.vector.tensor_tensor(o[:, blocks(s), :], scratch(x_).rearrange("p (b m) -> p b m", b=BPS),
                                            attn_in[:, q, blocks(s), :], ALU.add).then_inc(s_read[BANK[x_][0]], 1)
                elif stage == "add_attn":
                    q, r = a
                    lo, hi = ln_parts(2, q)[r]
                    dve.wait_ge(s_norm[2], 2 * q + hi // BPS)
                    dve.wait_ge(s_x1in, 16 * (q + 1))
                    nc.vector.tensor_tensor(x1[:, lo:hi, :], x1[:, lo:hi, :], normed[:, lo:hi, :],
                                            ALU.add).then_inc(s_x1, 1)
                elif stage == "ffn_up":
                    q, s, c = a
                    if q == 0:
                        dve.wait_ge(s_hsilu, 3 * s + c + 1)
                    else:
                        was_read(dve, ("ffn_gate", q, s, c))
                    written(dve, x_)
                    nc.vector.tensor_tensor(hid(s, c), scratch(x_), hid(s, c),
                                            ALU.mult).then_inc(s_read[BANK[x_][0]], 1)
                elif stage == "add_ffn":
                    q, r = a
                    lo, hi = ln_parts(4, q)[r]
                    dve.wait_ge(s_norm[4], 2 * q + hi // BPS)
                    dst = o if q == 0 else out_end
                    nc.vector.tensor_tensor(dst[:, lo:hi, :], x1[:, lo:hi, :], normed[:, lo:hi, :],
                                            ALU.add).then_inc(s_x2, 1)


def kernel(**inputs):
    import numpy as np
    import concourse.bacc as bacc
    from concourse.bass_utils import run_bass_kernel_spmd

    w = {n[len("L0_"):]: np.asarray(a) for n, a in inputs.items()}
    dirs = ("attn_f_", "attn_b_")

    def halves(a):
        return a.reshape((2, P) + a.shape[1:])

    packed = np.zeros((P, NCOLS), np.float32)

    def put(name, a):
        packed[:, COLS[name][0]:COLS[name][1]] = a.reshape(P, -1)

    put("ident", np.eye(P, dtype=np.float32))
    put("rev", np.eye(P, dtype=np.float32)[::-1])
    put("gamma", w["attn_gamma"])
    put("beta", w["attn_beta"])
    for name, key in (("conv_b", "conv_b"), ("skip", "D"), ("a_log", "A_log")):
        put(name, np.stack([np.moveaxis(halves(w[d + key]), 1, 0) for d in dirs], 1))
    sel = np.zeros((P, NS), np.float32)
    for row in (ROW_HI, ROW_LO, ROW_MID):
        sel[row + np.arange(NS), np.arange(NS)] = 1
    put("sel", sel)
    put("wz", np.stack([w[d + "in_w"][DI:].T for d in dirs], 1))
    wx = np.zeros((P, 2, 2, XROWS), np.float32)
    for n, d in enumerate(dirs):
        xp = np.moveaxis(halves(w[d + "xproj_w"].T), 1, 0)
        for row in (ROW_HI, ROW_LO, ROW_MID):
            wx[:, n, :, row:row + NS] = xp[:, :, RANK:RANK + NS]
        wx[:, n, :, NS:2 * NS] = xp[:, :, RANK + NS:]
        wx[:, n, :, ROW_DT:XROWS] = xp[:, :, :RANK]
    put("wx", wx)
    put("wo", np.stack([np.moveaxis(halves(w[d + "out_w"].T), 1, 0) for d in dirs], 1))
    wdt = np.zeros((P, 2, DI), np.float32)
    for n, d in enumerate(dirs):
        wdt[ROW_DT:XROWS, n] = w[d + "dt_w"].T
        wdt[XROWS, n] = w[d + "dt_b"]
    put("wdt", wdt)
    taps = np.stack([np.broadcast_to(w[d + "conv_w"][:, 0, :].T, (P, TAPS, DI)) for d in dirs], 1)
    w_u = np.stack([w[d + "in_w"][:DI].T for d in dirs], 1)
    w_down = np.moveaxis(w["ffn_w_down"].T.reshape(3, P, DM), 1, 0).reshape(P, HID)
    w_ffn = np.concatenate([w["ffn_w_gate"].T, w["ffn_w_up"].T, w_down], 1)

    nc = bacc.Bacc("TRN2", target_bir_lowering=False, num_devices=1)
    arrays = {"x": w["attn_x"], "packed": packed, "conv_taps": taps, "w_u": w_u, "w_ffn": w_ffn}
    arrays = {n + "_dram": np.ascontiguousarray(a) for n, a in arrays.items()}
    args = [nc.dram_tensor(n, a.shape, mybir.dt.from_np(a.dtype), kind="ExternalInput").ap()
            for n, a in arrays.items()]
    args.append(nc.dram_tensor("c_rows_dram", (UNITS, NS, PT), F32, kind="Internal").ap())
    args.append(nc.dram_tensor("out_0_dram", (BATCH, SEQ, DM), F32, kind="ExternalOutput").ap())
    mamba_sandwich(nc, *args)
    r = run_bass_kernel_spmd(nc, [arrays], core_ids=[0])
    return r.results[0]["out_0_dram"]
```

```python
from contextlib import ExitStack

import concourse.bass as bass
from concourse import mybir

P = 128
BATCH, SEQ, DM = 4, 512, 128
DI, NS, RANK, TAPS = 256, 16, 8, 4
HID = 384
PAIRS = 2
PT = BATCH // PAIRS * SEQ
BLK = PT // P
BPS = SEQ // P
UNITS = 2 * PAIRS
SEGS = 2 * UNITS
STEPS = SEGS * NS
EPS = 1e-5

ROW_HI, ROW_LO, ROW_MID, ROW_DT = 0, 32, 64, 96
XROWS = ROW_DT + RANK
COLS = {}
_at = 0
for _name, _n in (("ident", P), ("rev", P), ("gamma", 1), ("beta", 1), ("conv_b", 4), ("skip", 4),
                  ("conv_w", TAPS), ("a_log", 4 * NS), ("sel", NS), ("wz", 2 * DI), ("wx", 4 * XROWS),
                  ("wo", 4 * DM), ("wdt", 2 * DI)):
    COLS[_name] = (_at, _at + _n)
    _at += _n
NCOLS = _at

DA_RING, H_RING, BB_RING, C_RING = 4, 4, 2, 5
BANKS = 2 + 2 * BB_RING

ALU = mybir.AluOpType
ACT = mybir.ActivationFunctionType
F32 = mybir.dt.float32
BF16 = mybir.dt.bfloat16
I32 = mybir.dt.int32


def state_of(i):
    k, h, p = i // (2 * NS), i // NS % 2, i % NS
    return p if (k + h) % 2 == 0 else NS - 1 - p


def plan_c_loads():
    keys = [(i // (2 * NS), state_of(i)) for i in range(STEPS)]
    loads, slots, held, last = [], [], [None] * C_RING, [-1] * C_RING

    def next_use(key, i):
        return next((n for n in range(i, STEPS) if keys[n] == key), STEPS)

    for i, key in enumerate(keys):
        if key not in held:
            idle = [n for n in range(C_RING) if held[n] is None or last[n] < i - 2]
            slot = max(idle, key=lambda n: next_use(held[n], i) if held[n] else 2 * STEPS)
            loads.append((*key, slot, i, last[slot]))
            held[slot] = key
        slots.append(held.index(key))
        last[slots[-1]] = i
    return loads, slots


WHOLE, BY_SEQ = ((0, BLK),), ((0, BPS), (BPS, BLK))


def ln_parts(w, q):
    return BY_SEQ if (w < 2 and q == 0) or (w >= 2 and q == PAIRS - 1) else WHOLE


def ln_count(w, q, r):
    return sum(len(ln_parts(w, n)) for n in range(q)) + r + 1


def norm_stages(w, q, r=0, on_act=False):
    lo, hi = ln_parts(w, q)[r]
    sequences = range(lo // BPS, hi // BPS)
    rsqrt = [("ln_var", w, q, r), ("ln_pow", w, q, r)]
    apply = [("ln_shift", w, q, r)] + [("ln_act", w, q, s) for s in sequences]
    if ln_parts(w, q) == WHOLE:
        return [(stage, w, q, s) for stage in ("ln_mean", "ln_square") for s in sequences] + rsqrt + apply
    stats = [("ln_stats", w, q, s) for s in sequences]
    return stats + rsqrt + (apply if on_act else [("ln_dve", w, q, r)])


SLOTS = {
    "turn 0": (0, 0),
    "norm 0": (0, 0, 0, 0, 3, 5, 8, 8, 11),
    "norm 1": (10, 12, 13, 14, 16, 17, 19, 21, 24),
    "turn 1": (28, 33, 45, 48),
    "taps 1": (2, 3, 5, 5, 5, 8, 8, 9, 11, 11, 12, 13, 14, 15, 15, 17),
    "silu_u 1": (18,),
    "xproj 1": (19, 21, 21, 23, 23, 23, 23, 24),
    "split 1": (26, 27),
    "dt 1 0": (25, 26, 26, 27, 28, 27, 28, 29, 29, 29),
    "taps 2": (29, 30, 33, 34, 35, 36, 37, 38, 39, 40, 40, 41, 42, 42, 44, 45),
    "silu_u 2": (46,),
    "xproj 2": (50, 50, 51, 52, 52, 52, 52, 55),
    "split 2": (54, 57),
    "dt 2 0": (53, 56, 56, 56, 58, 57, 58, 58, 59, 61),
    "taps 3": (59, 60, 60, 61, 64, 65, 66, 66, 68, 68, 69, 71, 72, 73, 74, 76),
    "silu_u 3": (77,),
    "xproj 3": (81, 81, 81, 82, 82, 82, 83, 83),
    "split 3": (84, 84),
    "dt 3 0": (84, 85, 85, 87, 87, 87, 88, 89, 89, 91),
    "dt 0 1": (3, 4, 4, 6, 7, 6, 8, 9, 10, 13),
    "z 0": (10, 11, 12, 17, 18),
    "gate 0": (24, 25, 27, 27),
    "gate 1": (35, 37, 38, 38),
    "dt 1 1": (30, 31, 32, 32, 35, 34, 35, 35, 38, 40),
    "z 1": (39, 40, 44, 46, 51),
    "gate 2": (59, 59, 61, 61),
    "gate 3": (67, 68, 70, 70),
    "dt 2 1": (62, 62, 64, 64, 65, 65, 65, 65, 67, 69),
    "z 2": (60, 65, 69, 71, 71),
    "gate 4": (87, 87, 91, 92),
    "gate 5": (99, 99, 100, 101),
    "dt 3 1": (88, 90, 91, 92, 94, 92, 95, 97, 98, 104),
    "z 3": (94, 94, 101, 104, 104),
    "gate 6": (114, 114, 117, 117),
    "oproj": (77, 77, 79, 80, 80, 85, 87, 87, 87, 88),
    "norm 2": (84, 91, 91, 91, 92, 92, 94, 95, 95, 97),
    "norm 3": (98, 98, 98, 98, 99, 99, 101, 102, 103, 103, 103),
    "ffn_gate": (104, 105, 107, 107, 109, 110, 111),
    "ffn_up": (113, 118, 121, 122, 123, 124),
    "ffn_down": (120, 121, 122, 122, 125, 125, 127, 129),
    "oproj_part": (116, 117, 118, 119, 120, 124, 124, 126, 126, 129),
}


def plan():
    woven = {i: [] for i in range(STEPS + 2)}

    def put(slot, *items):
        woven[slot].extend(items)

    def spread(name, items):
        for slot, item in zip(SLOTS[name], items, strict=True):
            put(slot, item)

    def taps(k):
        for h in range(2):
            for s in range(2):
                for t in range(TAPS):
                    yield ("tap", k, h, s, t)

    def half(k, h):
        return [("dt", k, h, 0), ("dt", k, h, 1)] + [(stage, k, h) for stage in (
            "sp_exp", "sp_one", "sp_rest", "sp_ln", "skip", "dt_sub", "dt_add", "dtu")]

    def blockwise(stage, q):
        return [x for s in range(2) for x in [*((stage + "_mm", q, s, b) for b in range(BPS)), (stage, q, s)]]

    (st0, va0, po0, ap0), (st1, va1, po1, ap1) = (norm_stages(0, 0, r) for r in range(2))
    (st2, va2, po2, ap2), (st3, va3, po3, ap3) = (norm_stages(1, 0, r) for r in range(2))
    start = [st0, va0, po0, st1, va1, po1, ap0, st2, va2, po2, ap1, ap2, ("fold_taps", 0), st3, va3, po3, ap3]
    first_taps, second_taps = ([("tap", 0, 0, s, t) for t in range(TAPS)] for s in range(2))
    start += [("turn", 0, 0, 0), ("u_mm", 0), ("conv", 0), ("fold_taps", 1), ("ffn_weights",), *first_taps[:-1],
              ("conv_silu", 0), ("turn", 0, 0, 1), first_taps[-1], ("conv_out", 0, 0, 0), ("u_mm", 1),
              ("conv", 1), *second_taps, ("conv_out", 0, 0, 1), ("conv_silu", 1)]
    for s in range(2):
        start += [("xproj_mm", 0, s, 0), ("xproj_mm", 0, s, 1), ("xproj", 0, s), ("dt_rows", s), ("xproj_low", 0, s)]
    start += [("dt", 0, 0, 0), ("sp_exp", 0, 0, 0), ("split_mid",), ("dt", 0, 0, 1), ("sp_exp", 0, 0, 1),
              ("sp_one", 0, 0, 0), ("sp_one", 0, 0, 1), ("split", 0)]
    for stage in ("sp_rest", "sp_ln", "dt_sub"):
        start += [(stage, 0, 0, s) for s in range(2)]
    start += [("split_low", 0), ("exp_a",)]
    start += [("dt_add", 0, 0, 0), ("dt_add", 0, 0, 1), ("dtu", 0, 0, 0), ("neg_a",), ("dtu", 0, 0, 1)]
    start += [("exp", 0), ("exp", 1), ("skip", 0, 0), ("exp", 2), ("bcast", 0), ("bcast", 1),
              ("mul_b", 0)]

    spread("turn 0", [("turn", 0, 1, s) for s in range(2)])
    spread("norm 0", norm_stages(0, 1))
    spread("norm 1", norm_stages(1, 1))
    spread("turn 1", [("turn", 1, d, s) for d in range(2) for s in range(2)])
    for kn in range(1, UNITS):
        for slot, tap in zip(SLOTS[f"taps {kn}"], taps(kn), strict=True):
            put(slot, tap)
            if tap[4] == TAPS - 1:
                put(slot, ("conv_out",) + tap[1:4])
        spread(f"silu_u {kn}", [("silu_u", kn)])
        spread(f"xproj {kn}", [x for s in range(2) for x in (("xproj_mm", kn, s, 0), ("xproj_mm", kn, s, 1),
                                                             ("xproj", kn, s), ("xproj_low", kn, s))])
        spread(f"split {kn}", [("split", kn), ("split_low", kn)])
        spread(f"dt {kn} 0", half(kn, 0))
    for k in range(UNITS):
        spread(f"dt {k} 1", half(k, 1))
        spread(f"z {k}", [("z", k, h, s) for h in range(2) for s in range(2)] + [("silu_z", k)])
        for j in range(2 * k, min(2 * k + 2, SEGS - 1)):
            spread(f"gate {j}", [(stage, j, s) for s in range(2) for stage in ("back", "gate")])
    spread("oproj", blockwise("oproj", 0))
    spread("norm 2", norm_stages(2, 0) + [("add_attn", 0, 0)])
    spread("norm 3", norm_stages(3, 0) + [("turn_x1", 0, s) for s in range(2)])
    spread("ffn_gate", [("ffn_gate", 0, s, c) for s in range(2) for c in range(3)] + [("ffn_silu", 0)])
    spread("ffn_up", [("ffn_up", 0, s, c) for s in range(2) for c in range(3)])
    spread("ffn_down", [x for s in range(2)
                        for x in [*(("ffn_down_mm", 0, s, c) for c in range(3)), ("ffn_down", 0, s)]])
    spread("oproj_part", blockwise("oproj_part", PAIRS - 1))

    order = list(start)
    for i in range(STEPS + 2):
        if i < STEPS:
            order += [("scan", i), ("mul_c", i)]
            if i >= 1 and i + 1 < STEPS:
                order.append(("bcast", i + 1))
            if i + 1 < STEPS:
                order.append(("mul_b", i + 1))
            if i + DA_RING - 1 < STEPS:
                order.append(("exp", i + DA_RING - 1))
        if i >= 2:
            f = i - 2
            if f % NS == 1:
                order += [("seed", f // NS), ("fold", f - 1)]
            if f % NS and f < STEPS - 1:
                order.append(("fold", f))
            if f % NS == NS - 1 and f < STEPS - 1:
                order += [("y_out", f // NS, s) for s in range(2)]
        order += woven[i]

    q = PAIRS - 1
    *stats4, var4, pow4, shift4, act4_first, act4_second = norm_stages(4, 0)
    for s in range(2):
        order += [("fold", STEPS - 1, s), ("y_out", SEGS - 1, s)]
    order += stats4 + [("oproj_base", s) for s in range(2)]
    order += [(stage, SEGS - 1, s) for stage in ("back", "gate") for s in range(2)]
    for s in range(2):
        order += [("oproj_mm", q, s, b) for b in range(BPS)]
    early, late = norm_stages(2, q, 0), norm_stages(2, q, 1, on_act=True)
    order += early[:3] + late[:3] + [var4, pow4, early[3], ("oproj", q, 0), *late[3:], ("oproj", q, 1)]
    order += [("add_attn", q, 0), shift4, act4_first, act4_second]
    early, late = norm_stages(3, q, 0), norm_stages(3, q, 1, on_act=True)
    order += early[:3] + [("add_attn", q, 1)] + late[:3] + early[3:] + [late[3], ("turn_x1", q, 0)] + late[4:]

    def ffn(stage, s):
        return [(stage, q, s, c) for c in range(3)]

    order += [*ffn("ffn_gate", 0), ("turn_x1", q, 1), ("add_ffn", 0, 0), *ffn("ffn_up", 0), *ffn("ffn_gate", 1),
              *ffn("ffn_down_mm", 0), *ffn("ffn_up", 1), *ffn("ffn_down_mm", 1)]
    early, late = norm_stages(4, q, 0, on_act=True), norm_stages(4, q, 1)
    order += early + [("ffn_down", q, 0)] + late[:3] + [("add_ffn", q, 0)]
    order += [late[3], ("ffn_down", q, 1), ("add_ffn", q, 1)]
    return order


PRODUCERS = {"conv": "u_mm", "conv_out": "tap", "xproj_low": "xproj_mm", "gate": "back", "oproj": "oproj_mm",
             "oproj_part": "oproj_part_mm", "ffn_down": "ffn_down_mm"}
SCRATCH = (*PRODUCERS, "turn", "z", "dt", "turn_x1", "ffn_gate", "ffn_up")


def plan_banks(order):
    readers = {m: stage for stage, m in PRODUCERS.items()}
    first, last = {}, {}
    for n, x in enumerate(order):
        key = (readers[x[0]],) + x[1:4 if x[0] == "tap" else 3] if x[0] in readers else x
        if key[0] in SCRATCH:
            first.setdefault(key, n)
            last[key] = n
    scanned = order.index(("fold", STEPS - 1, 1))
    banks, uses, busy = {}, [0] * BANKS, [-1] * BANKS
    for key in sorted(first, key=first.get):
        usable = range(BANKS if first[key] > scanned else 2)
        bank = min(usable, key=lambda n: busy[n])
        assert busy[bank] < first[key], key
        busy[bank] = last[key]
        uses[bank] += 1
        banks[key] = (bank, uses[bank])
    return banks


def mamba_sandwich(nc, x, packed, conv_taps, w_u, w_ffn, c_rows, out):
    ORDER = plan()
    BANK = plan_banks(ORDER)
    C_LOADS, C_SLOT = plan_c_loads()
    c_need, c_count = {}, [0] * C_RING
    for k, n, slot, step, _ in C_LOADS:
        c_count[slot] += 1
        c_need[step] = (slot, 16 * c_count[slot])

    with ExitStack() as ctx:
        def sb(name, shape, dt=F32):
            return ctx.enter_context(nc.sbuf_tensor(name, shape, dt))

        def sem(name):
            return ctx.enter_context(nc.semaphore(name))

        bb = ctx.enter_context(nc.psum_tensor("bb", [P, BB_RING, PT], F32))
        ysum = ctx.enter_context(nc.psum_tensor("ysum", [P, PT], F32))
        scr = ctx.enter_context(nc.psum_tensor("scr", [P, 2, SEQ], F32))

        wts = sb("wts", [P, NCOLS])
        wconv = sb("wconv", [P, 2, TAPS, DI])
        neg_a = sb("neg_a", [P, 4 * NS])
        sel = sb("sel", [ROW_DT, NS, P], BF16)
        wffn = sb("wffn", [P, 3 * HID])
        stats = sb("stats", [P, 5, PAIRS, BLK, 6])
        mean_var = sb("mean_var", [P, 5, PAIRS, BLK, 2])
        rstd = sb("rstd", [P, 5, PAIRS, BLK])
        shift = sb("shift", [P, 5, PAIRS, BLK])
        minus_half = sb("minus_half", [P, BLK])
        x0 = sb("x0", [P, BLK, DM])
        attn_in = sb("attn_in", [P, PAIRS, BLK, DM])
        normed = sb("normed", [P, BLK, DM])
        x1 = sb("x1", [P, BLK, DM])
        o = sb("o", [P, BLK, DM])
        PAD = TAPS - 1
        xn_fwd = sb("xn_fwd", [P, PAIRS, 2, PAD + SEQ])
        xn_rev = sb("xn_rev", [P, 2, PAD + SEQ])
        u = sb("u", [P, 2, PT])
        zs = sb("zs", [P, 2, PT])
        skip = sb("skip", [P, 2, PT])
        parts = sb("parts", [ROW_DT, 2, PT], BF16)
        xdbl = sb("xdbl", [P, PT])
        dt = sb("dt", [P, 3, PT])
        dtu = sb("dtu", [P, 3, PT])
        work = sb("work", [P, 3 * PT])
        da = sb("da", [P, DA_RING, 2, SEQ])
        hq = sb("hq", [P, H_RING, PT])
        c_tiles = sb("c_tiles", [P, C_RING, PT])
        y_t = sb("y_t", [P, PT])
        gated = sb("gated", [P, 2, 2, PT])

        def by_block(tile):
            return tile.rearrange("p (b m) -> p b m", b=BLK)

        e = work[:, 0:PT]
        ln_one = work[:, PT:2 * PT]
        tmp = work[:, 2 * PT:3 * PT]
        x1_t = work[:, 0:PT]
        hid_first = [work[:, PT + c * SEQ:PT + (c + 1) * SEQ] for c in range(3)]
        rest = tmp
        mid_lo = xdbl[ROW_LO:ROW_LO + 32, 0:PT // 2].bitcast(BF16)
        w_u_stage = gated[:, 0, 0, 0:2 * DI].rearrange("p (d e) -> p d e", d=2)
        ffn_stage = gated[:, 1].rearrange("p h t -> p (h t)")[:, 0:3 * HID].bitcast(I32)
        hid_second = [xn_rev[:, 0, 0:SEQ], xn_rev[:, 1, 0:SEQ], xn_fwd[:, 0, 0, 0:SEQ]]
        x1_of = [x1, by_block(xdbl[:])]
        normed_of = [normed, by_block(skip[:, 1])]
        out_of = [o, x0]

        def col(name):
            return wts[:, COLS[name][0]:COLS[name][1]]

        ident, rev = col("ident"), col("rev")
        wz = col("wz").rearrange("p (d e) -> p d e", d=2)
        wx = col("wx").rearrange("p (d h r) -> p d h r", d=2, h=2)
        wo = col("wo").rearrange("p (d h m) -> p d h m", d=2, h=2)
        wdt = col("wdt").rearrange("p (d e) -> p d e", d=2)
        perm = [ident, rev]
        w_gate, w_up, w_down = (wffn[:, n * HID:(n + 1) * HID] for n in range(3))

        def vec(name, d, h):
            c = COLS[name][0] + 2 * d + h
            return wts[:, c:c + 1]

        s_x0 = [sem("x0_first_loaded"), sem("x0_second_loaded")]
        s_x1in = sem("x1_holds_x0")
        s_w = sem("packed_loaded")
        s_wc = [sem("fwd_taps_loaded"), sem("rev_taps_loaded")]
        s_wf = sem("ffn_weights_loaded")
        s_zero = sem("zeros_set")
        s_wconv = sem("conv_folded")
        s_wffn = sem("ffn_dequantised")
        s_expa = sem("exp_a_log_done")
        s_nega = sem("neg_a_done")
        s_sel = sem("selector_done")
        s_full = [sem(f"scratch{n}_written") for n in range(BANKS)]
        s_read = [sem(f"scratch{n}_read") for n in range(BANKS)]
        s_bcast = sem("b_broadcast")
        s_dbu = sem("dbu_done")
        s_exp = sem("da_done")
        s_scan = sem("scan_done")
        s_q = sem("c_product_done")
        s_fold = sem("state_summed")
        s_seed = sem("skip_seeded")
        s_yout = sem("y_copied")
        s_cl = [sem(f"c_tile{n}_loaded") for n in range(C_RING)]
        s_cst = sem("c_rows_stored")
        s_high = sem("high_parts_done")
        s_dtrows = sem("dt_rows_copied")
        s_crows = sem("c_rows_copied")
        s_conv = sem("conv_step_done")
        s_csilu = sem("second_half_silu_done")
        s_mid = sem("middle_parts_done")
        s_parts = sem("b_parts_done")
        s_silu_u = sem("u_silu_done")
        s_silu_z = sem("z_silu_done")
        s_spexp = sem("softplus_exp_done")
        s_sprest = sem("softplus_rest_done")
        s_sub = sem("softplus_rest_taken_off")
        s_spln = sem("softplus_ln_done")
        s_dt = sem("dt_done")
        s_dtu = sem("dtu_done")
        s_skip = sem("skip_done")
        s_stat = [sem(f"ln{w}_stats_done") for w in range(5)]
        s_var = [sem(f"ln{w}_var_done") for w in range(5)]
        s_pow = [sem(f"ln{w}_rstd_done") for w in range(5)]
        s_shift = [sem(f"ln{w}_shift_done") for w in range(5)]
        s_norm = [sem(f"ln{w}_applied") for w in range(5)]
        s_x1 = sem("x1_done")
        s_hsilu = sem("gate_silu_done")
        s_x2 = sem("x2_done")
        s_out = sem("out_stored")
        s_one = sem("one_plus_e_done")
        s_abs = sem("softplus_abs_done")
        s_ones = sem("ones_row_set")
        s_half = sem("minus_half_set")

        x_tok = x.rearrange("s (b p) m -> p s b m", p=P)
        out_tok = out.rearrange("s (b p) m -> p s b m", p=P)

        def pair_of(ap, q):
            return ap[:, 2 * q:2 * q + 2, :, :]

        def by_seq(tile):
            return tile.rearrange("p (s b) m -> p s b m", s=2)

        def scratch(stage):
            bank = BANK[stage][0]
            return scr[:, bank, :] if bank < 2 else bb[:, (bank - 2) // 2, tok(bank % 2)]

        def may_write(eng, stage):
            b, n = BANK[stage]
            if n > 1:
                eng.wait_ge(s_read[b], n - 1)

        def written(eng, stage):
            b, n = BANK[stage]
            eng.wait_ge(s_full[b], n)

        def was_read(eng, stage):
            b, n = BANK[stage]
            eng.wait_ge(s_read[b], n)

        def tok(s):
            return slice(s * SEQ, (s + 1) * SEQ)

        def part(a):
            return tok(a[2]) if len(a) > 2 else slice(0, PT)

        def size(a):
            return 1 if len(a) > 2 else 2

        def upto(a):
            return 4 * a[0] + 2 * a[1] + (a[2] + 1 if len(a) > 2 else 2)

        def before(a):
            return 4 * a[0] + 2 * a[1]

        def u_ready(eng, k, sequences=range(2), halves=range(2)):
            if k == 0:
                for s in sequences:
                    was_read(eng, ("conv_out", 0, 0, s))
                    if 1 in halves:
                        eng.wait_ge(s_csilu, s + 1)
            else:
                eng.wait_ge(s_silu_u, k)

        def one_plus(a):
            return y_t if a[:2] == (0, 0) else tmp

        def on_pool(k, h, *s):
            return h == 1 or k >= 2

        def soft_plus(engine, wait_on, stage, *a):
            k, h = a[:2]
            g = dt[:, (2 * k + h) % 3, part(a)]
            if stage == "dt_sub":
                wait_on.wait_ge(s_sprest, upto(a))
                was_read(wait_on, ("dt", k, h, a[2] if len(a) > 2 else 1))
                engine.tensor_tensor(g, g, one_plus(a)[:, part(a)], ALU.subtract).then_inc(s_sub, size(a))
            else:
                wait_on.wait_ge(s_spln, upto(a))
                wait_on.wait_ge(s_sub, upto(a))
                engine.tensor_tensor(g, g, ln_one[:, part(a)], ALU.add).then_inc(s_dt, size(a))

        def blocks(s):
            return slice(s * BPS, (s + 1) * BPS)

        def hid(s, c):
            return (hid_first, hid_second)[s][c]

        def ln_in(w, q, b):
            if in_scratch(w, q):
                return scratch(made_by(w, q, b // BPS))[:, (b % BPS) * P:(b % BPS + 1) * P]
            return (x0, attn_in[:, q], o, x1_of[q], o)[w][:, b, :]

        def ln_out(w, q, b):
            return (attn_in[:, q], normed, *3 * [normed_of[q]])[w][:, b, :]

        def ln_in_ready(eng, w, q, s):
            if w == 0:
                eng.wait_ge(s_x0[s], 16 * (q + 1))
            elif w == 1:
                eng.wait_ge(s_norm[0], 2 * q + s + 1)
            elif w == 3:
                eng.wait_ge(s_x1, 1 if q == 0 else 2 + s)
            elif in_scratch(w, q):
                written(eng, made_by(w, q, s))
            else:
                was_read(eng, made_by(w, q, s))

        def made_by(w, q, s):
            return ("oproj" if w == 2 else "ffn_down", q, s)

        def in_scratch(w, q):
            return w in (2, 4) and q == PAIRS - 1

        def signal_norm(ins, w, q, s):
            ins.then_inc(s_read[BANK[made_by(w, q, s)][0]] if in_scratch(w, q) else s_norm[w], 1)

        def normed_ready(eng, w, q, s):
            if in_scratch(w, q):
                was_read(eng, made_by(w, q, s))
            else:
                eng.wait_ge(s_norm[w], 2 * q + s + 1)

        block = ctx.enter_context(nc.Block())

        @block.sync
        def _(sp):
            for s in range(2):
                sp.dma_start(x0[:, s * BPS:(s + 1) * BPS, :], x_tok[:, s]).then_inc(s_x0[s], 16)
            sp.dma_start(wts[:], packed).then_inc(s_w, 16)
            for d in range(2):
                sp.dma_start(w_u_stage[:, d], w_u[:, d]).then_inc(s_wc[d], 16)
                sp.dma_start(wconv[:, d], conv_taps[:, d]).then_inc(s_wc[d], 16)
            sp.dma_start(ffn_stage, w_ffn).then_inc(s_wf, 16)
            sp.dma_start(by_seq(x1[:]), pair_of(x_tok, 0)).then_inc(s_x1in, 16)
            sp.wait_ge(s_norm[0], ln_count(0, 0, 1))
            for s in range(2):
                sp.dma_start(x0[:, s * BPS:(s + 1) * BPS, :], x_tok[:, 2 + s]).then_inc(s_x0[s], 16)
            stored = -1
            for k, n, slot, step, free in C_LOADS:
                if k > stored:
                    sp.wait_ge(s_crows, 2 * (k + 1))
                    sp.dma_start(c_rows[k], xdbl[NS:2 * NS, :]).then_inc(s_cst, 16)
                    sp.wait_ge(s_cst, 16 * (k + 1))
                    stored = k
                if free >= 0:
                    sp.wait_ge(s_q, free + 1)
                sp.dma_start(c_tiles[:, slot, :], c_rows[k, n].partition_broadcast(P)).then_inc(s_cl[slot], 16)
            sp.wait_ge(s_parts, UNITS)
            was_read(sp, ("dt", UNITS - 1, 1, 1))
            sp.dma_start(by_seq(x1_of[1]), pair_of(x_tok, 1)).then_inc(s_x1in, 16)
            sp.wait_ge(s_x2, 1)
            sp.dma_start(pair_of(out_tok, 0), by_seq(o[:])).then_inc(s_out, 16)
            for s in range(2):
                sp.wait_ge(s_x2, 2 + s)
                sp.dma_start(out_tok[:, 2 + s], out_of[1][:, s * BPS:(s + 1) * BPS, :]).then_inc(s_out, 16)
            sp.wait_ge(s_out, 48)

        @block.tensor
        def _(pe):
            def residual(use, b, first):
                q, s = use[1:]
                nc.tensor.matmul(scratch(use)[:, b * P:(b + 1) * P], ident, attn_in[:, q, s * BPS + b, :],
                                 start=first, stop=False, skip_group_check=True)

            pe.wait_ge(s_w, 16)
            for item in ORDER:
                stage, a = item[0], item[1:]
                if stage == "bcast":
                    i, = a
                    k = i // (2 * NS)
                    if i == 0:
                        pe.wait_ge(s_sel, 1)
                    if i % (2 * NS) == 0:
                        pe.wait_ge(s_parts, k + 1)
                    if i >= BB_RING:
                        pe.wait_ge(s_scan, i - BB_RING + 1)
                    n = state_of(i)
                    for s in range(2):
                        mm = nc.tensor.matmul(bb[:, i % BB_RING, tok(s)], sel[:, n, :], parts[:, k % 2, tok(s)],
                                              start=True, stop=True)
                    mm.then_inc(s_bcast, 1)
                elif stage == "seed":
                    j, = a
                    pe.wait_ge(s_skip, j + 1)
                    if j >= 1:
                        pe.wait_ge(s_yout, 2 * j)
                    for b in range(BLK):
                        mm = nc.tensor.matmul(ysum[:, b * P:(b + 1) * P], skip[:, j % 2, b * P:(b + 1) * P],
                                              ident, start=(b % BPS == 0), stop=False, is_transpose=True,
                                              skip_group_check=True)
                    mm.then_inc(s_seed, 1)
                elif stage == "fold":
                    i, done = a[0], a[1:] or (1,)
                    pe.wait_ge(s_q, i + 1 + (done[0] if len(a) > 1 else 0))
                    for b in range(BLK) if len(a) == 1 else range(done[0] * BPS, (done[0] + 1) * BPS):
                        mm = nc.tensor.matmul(ysum[:, b * P:(b + 1) * P], hq[:, i % H_RING, b * P:(b + 1) * P],
                                              ident, start=False, stop=(i % NS == NS - 1), is_transpose=True,
                                              skip_group_check=True)
                    mm.then_inc(s_fold, 1)
                elif stage == "back":
                    j, s = a
                    use = ("gate", j, s)
                    pe.wait_ge(s_yout, 2 * j + s + 1)
                    may_write(pe, use)
                    d = j // 2 % 2
                    for b in range(BPS):
                        src = s * BPS + (BPS - 1 - b if d else b)
                        mm = nc.tensor.matmul(scratch(use)[:, b * P:(b + 1) * P], y_t[:, src * P:(src + 1) * P],
                                              perm[d], start=True, stop=True, is_transpose=True)
                    mm.then_inc(s_full[BANK[use][0]], 1)
                elif stage == "turn":
                    q, d, s = a
                    pe.wait_ge(s_norm[1], 2 * q + s + 1)
                    may_write(pe, item)
                    for b in range(BPS):
                        src = s * BPS + (BPS - 1 - b if d else b)
                        mm = nc.tensor.matmul(scratch(item)[:, b * P:(b + 1) * P], normed[:, src, :],
                                              perm[d], start=True, stop=True, is_transpose=True)
                    mm.then_inc(s_full[BANK[item][0]], 1)
                elif stage == "tap":
                    k, h, s, t = a
                    q, d = k // 2, k % 2
                    use = ("conv_out", k, h, s)
                    if t == 0:
                        pe.wait_ge(s_wconv, d + 1)
                        pe.wait_ge(s_zero, 1)
                        was_read(pe, ("turn", q, d, s))
                        may_write(pe, use)
                    src = xn_rev[:, s, t:t + SEQ] if d else xn_fwd[:, q, s, t:t + SEQ]
                    mm = nc.tensor.matmul(scratch(use), wconv[:, d, t, h * P:(h + 1) * P], src,
                                          start=(t == 0), stop=(t == TAPS - 1))
                    if t == TAPS - 1:
                        mm.then_inc(s_full[BANK[use][0]], 1)
                elif stage == "u_mm":
                    s, = a
                    use = ("conv", s)
                    pe.wait_ge(s_wc[0], 32)
                    was_read(pe, ("turn", 0, 0, s))
                    may_write(pe, use)
                    nc.tensor.matmul(scratch(use), w_u_stage[:, 0, P:2 * P], xn_fwd[:, 0, s, PAD:PAD + SEQ],
                                     start=True, stop=True).then_inc(s_full[BANK[use][0]], 1)
                elif stage == "z":
                    k, h, s = a
                    q, d = k // 2, k % 2
                    was_read(pe, ("turn", q, 0, s))
                    may_write(pe, item)
                    nc.tensor.matmul(scratch(item), wz[:, d, h * P:(h + 1) * P], xn_fwd[:, q, s, PAD:PAD + SEQ],
                                     start=True, stop=True).then_inc(s_full[BANK[item][0]], 1)
                elif stage == "xproj_mm":
                    k, s, h = a
                    use = ("xproj_low", k, s)
                    u_ready(pe, k, sequences=[s], halves=[h])
                    if h == 0:
                        may_write(pe, use)
                    mm = nc.tensor.matmul(scratch(use)[0:XROWS, :], wx[:, k % 2, h, :], u[:, h, tok(s)],
                                          start=(h == 0), stop=(h == 1))
                    if h == 1:
                        mm.then_inc(s_full[BANK[use][0]], 1)
                elif stage == "dt":
                    k, h, s = a
                    pe.wait_ge(s_dtrows, 2 * k + s + 1)
                    pe.wait_ge(s_ones, 1)
                    may_write(pe, item)
                    rows = slice(ROW_DT, XROWS + 1)
                    nc.tensor.matmul(scratch(item), wdt[rows, k % 2, h * P:(h + 1) * P], xdbl[rows, tok(s)],
                                     start=True, stop=True).then_inc(s_full[BANK[item][0]], 1)
                elif stage in ("oproj_mm", "oproj_part_mm"):
                    q, s, b = a
                    use = (stage[:-len("_mm")], q, s)
                    segments = range(4)
                    if q == PAIRS - 1:
                        segments = range(3) if stage == "oproj_part_mm" else range(3, 4)
                    if b == 0:
                        was_read(pe, ("gate", 4 * q + segments[-1], s))
                        if use != ("oproj", PAIRS - 1, s):
                            may_write(pe, use)
                    at = slice((s * BPS + b) * P, (s * BPS + b + 1) * P)
                    if use != ("oproj", PAIRS - 1, s):
                        residual(use, b, b == 0)
                    for n in segments:
                        mm = nc.tensor.matmul(scratch(use)[:, b * P:(b + 1) * P], gated[:, n // 2, n % 2, at],
                                              wo[:, n // 2, n % 2, :], start=False, stop=(n == segments[-1]),
                                              skip_group_check=True)
                    if b == BPS - 1:
                        mm.then_inc(s_full[BANK[use][0]], 1)
                elif stage == "turn_x1":
                    q, s = a
                    pe.wait_ge(s_norm[3], 2 * q + s + 1)
                    may_write(pe, item)
                    for b in range(BPS):
                        mm = nc.tensor.matmul(scratch(item)[:, b * P:(b + 1) * P], normed_of[q][:, s * BPS + b, :],
                                              ident, start=True, stop=True, is_transpose=True)
                    mm.then_inc(s_full[BANK[item][0]], 1)
                elif stage in ("ffn_gate", "ffn_up"):
                    q, s, c = a
                    if c == 0 and stage == "ffn_gate":
                        pe.wait_ge(s_wffn, 1)
                        was_read(pe, ("turn_x1", q, s))
                    may_write(pe, item)
                    w = w_gate if stage == "ffn_gate" else w_up
                    nc.tensor.matmul(scratch(item), w[:, c * P:(c + 1) * P], x1_t[:, tok(s)],
                                     start=True, stop=True).then_inc(s_full[BANK[item][0]], 1)
                elif stage == "oproj_base":
                    s, = a
                    use = ("oproj", PAIRS - 1, s)
                    was_read(pe, ("oproj_part", PAIRS - 1, s))
                    may_write(pe, use)
                    for b in range(BPS):
                        residual(use, b, b == 0)
                elif stage == "ffn_down_mm":
                    q, s, c = a
                    use = ("ffn_down", q, s)
                    was_read(pe, ("ffn_up", q, s, c))
                    if c == 0:
                        may_write(pe, use)
                    for b in range(BPS):
                        mm = nc.tensor.matmul(scratch(use)[:, b * P:(b + 1) * P],
                                              hid(s, c)[:, b * P:(b + 1) * P],
                                              w_down[:, c * P:(c + 1) * P], start=(c == 0 and b == 0),
                                              stop=(c == 2), skip_group_check=True)
                    if c == 2:
                        mm.then_inc(s_full[BANK[use][0]], 1)

        @block.scalar
        def _(act):
            act.wait_ge(s_w, 16)
            nc.scalar.activation(sel[:], col("sel")[0:ROW_DT, :].unsqueeze(2).broadcast_to([ROW_DT, NS, P]),
                                 ACT.Copy).then_inc(s_sel, 1)
            for item in ORDER:
                stage, a = item[0], item[1:]
                if stage == "exp":
                    i, = a
                    j = i // NS
                    if i == 0:
                        act.wait_ge(s_nega, 1)
                        act.wait_ge(s_zero, 1)
                    if i % NS == 0:
                        act.wait_ge(s_dt, 2 * (j + 1))
                    if i >= DA_RING:
                        act.wait_ge(s_scan, i - DA_RING + 1)
                    c = (j % 4) * NS + state_of(i)
                    nc.scalar.activation(da[:, i % DA_RING, :, 1:SEQ],
                                         dt[:, j % 3, :].rearrange("p (s t) -> p s t", s=2)[:, :, 1:SEQ],
                                         ACT.Exp, scale=neg_a[:, c:c + 1]).then_inc(s_exp, 1)
                elif stage == "exp_a":
                    nc.scalar.activation(neg_a[:], col("a_log"), ACT.Exp).then_inc(s_expa, 1)
                elif stage == "y_out":
                    j, s = a
                    act.wait_ge(s_fold, NS * (j + 1) + (s if j == SEGS - 1 else 0))
                    if j >= 1:
                        written(act, ("gate", j - 1, s))
                    nc.scalar.activation(y_t[:, tok(s)], ysum[:, tok(s)], ACT.Copy).then_inc(s_yout, 1)
                elif stage == "turn":
                    q, d, s = a
                    written(act, item)
                    dst = xn_rev[:, s, PAD:] if d else xn_fwd[:, q, s, PAD:]
                    nc.scalar.activation(dst, scratch(item), ACT.Identity, scale=col("gamma"),
                                         bias=col("beta")).then_inc(s_read[BANK[item][0]], 1)
                elif stage == "conv_out":
                    k, h, s = a
                    written(act, item)
                    if k >= 1:
                        act.wait_ge(s_dtu, 2 * (2 * (k - 1) + h + 1))
                        act.wait_ge(s_skip, 2 * (k - 1) + h + 1)
                    nc.scalar.activation(u[:, h, tok(s)], scratch(item), ACT.Silu if k == 0 else ACT.Identity,
                                         bias=vec("conv_b", k % 2, h)).then_inc(s_read[BANK[item][0]], 1)
                elif stage == "conv_silu":
                    s, = a
                    was_read(act, ("conv", s))
                    nc.scalar.activation(u[:, 1, tok(s)], u[:, 1, tok(s)], ACT.Silu).then_inc(s_csilu, 1)
                elif stage == "z":
                    k, h, s = a
                    written(act, item)
                    if k >= 1:
                        was_read(act, ("gate", 2 * (k - 1) + h, s))
                    nc.scalar.activation(zs[:, h, tok(s)], scratch(item), ACT.Copy).then_inc(s_read[BANK[item][0]], 1)
                elif stage == "silu_u":
                    k, = a
                    for h in range(2):
                        for s in range(2):
                            was_read(act, ("conv_out", k, h, s))
                    nc.scalar.activation(u[:], u[:], ACT.Silu).then_inc(s_silu_u, 1)
                elif stage == "silu_z":
                    k, = a
                    for h in range(2):
                        for s in range(2):
                            was_read(act, ("z", k, h, s))
                    nc.scalar.activation(zs[:], zs[:], ACT.Silu).then_inc(s_silu_z, 1)
                elif stage == "xproj":
                    k, s = a
                    use = ("xproj_low", k, s)
                    written(act, use)
                    if k >= 1:
                        act.wait_ge(s_cst, 16 * k)
                    nc.scalar.activation(parts[:, k % 2, tok(s)], scratch(use)[0:ROW_DT, :],
                                         ACT.Copy).then_inc(s_high, 1)
                    if k >= 1:
                        nc.scalar.activation(xdbl[ROW_DT:XROWS, tok(s)], scratch(use)[ROW_DT:XROWS, :],
                                             ACT.Copy).then_inc(s_dtrows, 1)
                    nc.scalar.activation(xdbl[0:32, tok(s)], scratch(use)[0:32, :], ACT.Copy).then_inc(s_crows, 1)
                elif stage == "split":
                    k, = a
                    for s in range(2):
                        was_read(act, ("xproj_low", k, s))
                    nc.scalar.activation(mid_lo, rest[ROW_LO:ROW_LO + 32, :], ACT.Copy).then_inc(s_mid, 1)
                    if k >= 1:
                        rows = slice(ROW_MID, ROW_MID + 32)
                        nc.scalar.activation(parts[rows, k % 2, :], rest[rows, :], ACT.Copy).then_inc(s_mid, 1)
                elif stage == "dt":
                    k, h, s = a
                    written(act, item)
                    j = 2 * k + h
                    if j >= 1:
                        act.wait_ge(s_sprest, 2 * j)
                        act.wait_ge(s_spln, 2 * j)
                    if j >= 3:
                        act.wait_ge(s_dtu, 2 * (j - 2))
                    nc.scalar.activation(e[:, tok(s)], scratch(item), ACT.Abs).then_inc(s_abs, 1)
                    if j >= 1:
                        nc.scalar.activation(dt[:, j % 3, tok(s)], scratch(item),
                                             ACT.Relu).then_inc(s_read[BANK[item][0]], 1)
                elif stage == "sp_exp":
                    act.wait_ge(s_abs, upto(a))
                    nc.scalar.activation(e[:, part(a)], e[:, part(a)], ACT.Exp,
                                         scale=-1.0).then_inc(s_spexp, size(a))
                elif stage == "sp_one":
                    act.wait_ge(s_spexp, upto(a))
                    if a[:2] != (0, 0):
                        act.wait_ge(s_parts, a[0] + 1)
                        act.wait_ge(s_sub, before(a))
                    nc.scalar.activation(one_plus(a)[:, part(a)], e[:, part(a)], ACT.Identity,
                                         bias=1.0).then_inc(s_one, size(a))
                elif stage == "sp_ln":
                    if a[:2] != (0, 0):
                        act.wait_ge(s_dt, before(a))
                    nc.scalar.activation(ln_one[:, part(a)], e[:, part(a)], ACT.Ln,
                                         bias=1.0).then_inc(s_spln, size(a))
                elif stage == "skip":
                    k, h = a
                    u_ready(act, k)
                    if k >= 1:
                        act.wait_ge(s_seed, 2 * (k - 1) + h + 1)
                    nc.scalar.activation(skip[:, h, :], u[:, h, :], ACT.Copy,
                                         scale=vec("skip", k % 2, h)).then_inc(s_skip, 1)
                elif stage == "ln_mean":
                    w, q, s = a
                    ln_in_ready(act, w, q, s)
                    for b in range(s * BPS, (s + 1) * BPS):
                        nc.scalar.activation(ln_out(w, q, b), ln_in(w, q, b), ACT.Copy, scale=-1.0 / DM,
                                             accum_out=mean_var[:, w, q, b, 0:1]).then_inc(s_stat[w], 1)
                elif stage == "ln_square":
                    w, q, s = a
                    act.wait_ge(s_stat[w], 2 * BLK * q + BLK)
                    for b in range(s * BPS, (s + 1) * BPS):
                        nc.scalar.activation(ln_out(w, q, b), ln_in(w, q, b), ACT.Square,
                                             bias=mean_var[:, w, q, b, 0:1],
                                             accum_out=mean_var[:, w, q, b, 1:2]).then_inc(s_stat[w], 1)
                elif stage == "ln_act":
                    w, q, s = a
                    act.wait_ge(s_shift[w], q + 1 if w >= 2 else 1)
                    for b in range(s * BPS, (s + 1) * BPS):
                        ins = nc.scalar.activation(ln_out(w, q, b), ln_in(w, q, b), ACT.Identity,
                                                   scale=rstd[:, w, q, b:b + 1], bias=shift[:, w, q, b:b + 1])
                    signal_norm(ins, w, q, s)
                elif stage == "oproj_part" or stage == "oproj" and a[0] < PAIRS - 1:
                    q, s = a
                    written(act, item)
                    dst = attn_in[:, q] if stage == "oproj_part" else o
                    nc.scalar.activation(dst[:, blocks(s), :], scratch(item).rearrange("p (b m) -> p b m", b=BPS),
                                         ACT.Copy).then_inc(s_read[BANK[item][0]], 1)
                elif stage == "turn_x1" and a[0] < PAIRS - 1:
                    q, s = a
                    written(act, item)
                    act.wait_ge(s_dt, 2 * SEGS)
                    nc.scalar.activation(x1_t[:, tok(s)], scratch(item), ACT.Copy).then_inc(s_read[BANK[item][0]], 1)
                elif stage == "ffn_gate":
                    q, s, c = a
                    written(act, item)
                    nc.scalar.activation(hid(s, c), scratch(item), ACT.Copy if q == 0 else ACT.Silu
                                         ).then_inc(s_read[BANK[item][0]], 1)
                elif stage == "ffn_silu":
                    q, = a
                    for s in range(2):
                        for c in range(3):
                            was_read(act, ("ffn_gate", q, s, c))
                            nc.scalar.activation(hid(s, c), hid(s, c), ACT.Silu).then_inc(s_hsilu, 1)
                elif stage == "ffn_down" and a[0] < PAIRS - 1:
                    q, s = a
                    written(act, item)
                    nc.scalar.activation(o[:, blocks(s), :], scratch(item).rearrange("p (b m) -> p b m", b=BPS),
                                         ACT.Copy).then_inc(s_read[BANK[item][0]], 1)

        @block.gpsimd
        def _(pool):
            nc.gpsimd.memset(minus_half[:], -0.5).then_inc(s_half, 1)
            nc.gpsimd.memset(da[:, :, :, 0:1], 0.0)
            nc.gpsimd.memset(xn_rev[:, :, 0:PAD], 0.0)
            nc.gpsimd.memset(xn_fwd[:, :, :, 0:PAD], 0.0).then_inc(s_zero, 1)
            pool.wait_ge(s_half, 1)
            for item in ORDER:
                stage, a = item[0], item[1:]
                if stage == "mul_c":
                    i, = a
                    pool.wait_ge(s_scan, i + 1)
                    if i in c_need:
                        slot, n = c_need[i]
                        pool.wait_ge(s_cl[slot], n)
                    for at in (slice(0, PT),) if i < STEPS - 1 else (tok(0), tok(1)):
                        nc.gpsimd.tensor_tensor(hq[:, i % H_RING, at], hq[:, i % H_RING, at],
                                                c_tiles[:, C_SLOT[i], at], ALU.mult).then_inc(s_q, 1)
                elif stage in ("dt_sub", "dt_add") and on_pool(*a):
                    soft_plus(nc.gpsimd, pool, stage, *a)
                elif stage == "ln_pow":
                    w, q, r = a
                    pool.wait_ge(s_var[w], ln_count(w, q, r))
                    at = slice(*ln_parts(w, q)[r])
                    nc.gpsimd.tensor_tensor(rstd[:, w, q, at], rstd[:, w, q, at], minus_half[:, at],
                                            ALU.pow).then_inc(s_pow[w], 1)

        @block.vector
        def _(dve):
            nc.vector.memset(xdbl[ROW_DT:P, :], 1.0).then_inc(s_ones, 1)
            for item in ORDER:
                stage, a = item[0], item[1:]
                if stage == "mul_b":
                    i, = a
                    j = i // NS
                    dve.wait_ge(s_bcast, i + 1)
                    if i % NS == 0:
                        dve.wait_ge(s_dtu, 2 * (j + 1))
                    nc.vector.tensor_tensor(bb[:, i % BB_RING, :], bb[:, i % BB_RING, :], dtu[:, j % 3, :],
                                            ALU.mult).then_inc(s_dbu, 1)
                elif stage == "scan":
                    i, = a
                    dve.wait_ge(s_dbu, i + 1)
                    dve.wait_ge(s_exp, i + 1)
                    if i >= H_RING:
                        dve.wait_ge(s_fold, i - H_RING + 1)
                    nc.vector.tensor_tensor_scan(out=hq[:, i % H_RING, :],
                                                 data0=da[:, i % DA_RING].rearrange("p s t -> p (s t)"),
                                                 data1=bb[:, i % BB_RING, :], initial=0.0,
                                                 op0=ALU.mult, op1=ALU.add).then_inc(s_scan, 1)
                elif stage == "ln_stats":
                    w, q, s = a
                    ln_in_ready(dve, w, q, s)
                    for b in range(s * BPS, (s + 1) * BPS):
                        nc.vector.bn_stats(stats[:, w, q, b, :], ln_in(w, q, b)).then_inc(s_stat[w], 1)
                    done = 2 * BPS * (2 * q + s)
                    dve.wait_ge(s_stat[w], done + BPS)
                    for b in range(s * BPS, (s + 1) * BPS):
                        nc.vector.bn_aggr(mean_var[:, w, q, b, :], stats[:, w, q, b, :]).then_inc(s_stat[w], 1)
                elif stage == "ln_var":
                    w, q, r = a
                    lo, hi = ln_parts(w, q)[r]
                    dve.wait_ge(s_stat[w], 2 * (BLK * q + hi))
                    scale = 1.0 / DM if ln_parts(w, q) == WHOLE else 1.0
                    nc.vector.tensor_scalar(rstd[:, w, q, lo:hi], mean_var[:, w, q, lo:hi, 1], scale, EPS,
                                            ALU.mult, ALU.add).then_inc(s_var[w], 1)
                elif stage == "ln_shift":
                    w, q, r = a
                    dve.wait_ge(s_pow[w], ln_count(w, q, r))
                    at = slice(*ln_parts(w, q)[r])
                    sign = 1.0 if ln_parts(w, q) == WHOLE else -1.0
                    nc.vector.scalar_tensor_tensor(out=shift[:, w, q, at], in0=mean_var[:, w, q, at, 0], scalar=sign,
                                                   in1=rstd[:, w, q, at], op0=ALU.mult,
                                                   op1=ALU.mult).then_inc(s_shift[w], 1)
                elif stage == "ln_dve":
                    w, q, r = a
                    dve.wait_ge(s_pow[w], ln_count(w, q, r))
                    for b in range(*ln_parts(w, q)[r]):
                        ins = nc.vector.tensor_scalar(ln_out(w, q, b), ln_in(w, q, b),
                                                      mean_var[:, w, q, b, 0:1], rstd[:, w, q, b:b + 1],
                                                      ALU.subtract, ALU.mult)
                    signal_norm(ins, w, q, r)
                elif stage == "fold_taps":
                    d, = a
                    dve.wait_ge(s_wc[d], 32)
                    nc.vector.tensor_tensor(wconv[:, d], wconv[:, d],
                                            w_u_stage[:, d, :].unsqueeze(1).broadcast_to([P, TAPS, DI]),
                                            ALU.mult).then_inc(s_wconv, 1)
                elif stage == "neg_a":
                    dve.wait_ge(s_expa, 1)
                    nc.vector.tensor_scalar(neg_a[:], neg_a[:], -1.0, None, ALU.mult).then_inc(s_nega, 1)
                elif stage == "ffn_weights":
                    dve.wait_ge(s_wf, 16)
                    nc.vector.tensor_scalar(wffn[:], ffn_stage, 1.0 / 127.0, None, ALU.mult).then_inc(s_wffn, 1)
                elif stage == "xproj_low":
                    k, s = a
                    for copied in (s_high, s_dtrows, s_crows):
                        dve.wait_ge(copied, 2 * k + s + 1)
                    if k >= 1:
                        dve.wait_ge(s_sub, 4 * k)
                    nc.vector.tensor_tensor(rest[0:ROW_DT, tok(s)], scratch(item)[0:ROW_DT, :],
                                            parts[:, k % 2, tok(s)], ALU.subtract).then_inc(s_read[BANK[item][0]], 1)
                elif stage == "split_low":
                    k, = a
                    dve.wait_ge(s_mid, 2 * (k + 1))
                    rows = slice(ROW_LO, ROW_LO + 32)
                    nc.vector.tensor_tensor(parts[rows, k % 2, :], rest[rows, :], mid_lo,
                                            ALU.subtract).then_inc(s_parts, 1)
                elif stage == "split_mid":
                    for s in range(2):
                        was_read(dve, ("xproj_low", 0, s))
                    rows = slice(ROW_MID, ROW_MID + 32)
                    nc.vector.tensor_copy(parts[rows, 0, :], rest[rows, :]).then_inc(s_mid, 1)
                elif stage == "sp_rest":
                    dve.wait_ge(s_one, upto(a))
                    g = one_plus(a)[:, part(a)]
                    nc.vector.scalar_tensor_tensor(out=g, in0=g, scalar=-1.0, in1=e[:, part(a)], op0=ALU.add,
                                                   op1=ALU.subtract).then_inc(s_sprest, size(a))
                elif stage in ("dt_sub", "dt_add") and not on_pool(*a):
                    soft_plus(nc.vector, dve, stage, *a)
                elif stage == "dtu":
                    k, h = a[:2]
                    j = 2 * k + h
                    dve.wait_ge(s_dt, upto(a))
                    u_ready(dve, k, sequences=a[2:] or range(2), halves=[h])
                    nc.vector.tensor_tensor(dtu[:, j % 3, part(a)], dt[:, j % 3, part(a)], u[:, h, part(a)],
                                            ALU.mult).then_inc(s_dtu, size(a))
                elif stage == "conv":
                    s, = a
                    written(dve, item)
                    c = COLS["conv_w"][0]
                    for t in reversed(range(TAPS)):
                        back = TAPS - 1 - t
                        tap, dst = wts[:, c + t:c + t + 1], u[:, 1, s * SEQ + back:(s + 1) * SEQ]
                        src = scratch(item)[:, 0:SEQ - back]
                        if back == 0:
                            ins = nc.vector.tensor_scalar(dst, src, tap, vec("conv_b", 0, 1), ALU.mult, ALU.add)
                        else:
                            dve.wait_ge(s_conv, PAD * s + back)
                            ins = nc.vector.scalar_tensor_tensor(out=dst, in0=src, scalar=tap, in1=dst,
                                                                 op0=ALU.mult, op1=ALU.add)
                        ins.then_inc(s_conv if t else s_read[BANK[item][0]], 1)
                elif stage == "dt_rows":
                    s, = a
                    use = ("xproj_low", 0, s)
                    written(dve, use)
                    dve.wait_ge(s_ones, 1)
                    nc.vector.tensor_copy(xdbl[ROW_DT:XROWS, tok(s)],
                                          scratch(use)[ROW_DT:XROWS, :]).then_inc(s_dtrows, 1)
                elif stage == "dt" and a[:2] == (0, 0):
                    s = a[2]
                    dve.wait_ge(s_abs, s + 1)
                    nc.vector.tensor_scalar(dt[:, 0, tok(s)], scratch(item), 0.0, None,
                                            ALU.max).then_inc(s_read[BANK[item][0]], 1)
                elif stage == "gate":
                    j, s = a
                    q, d, h = j // 4, j // 2 % 2, j % 2
                    written(dve, item)
                    dve.wait_ge(s_silu_z, j // 2 + 1)
                    if q >= 1:
                        was_read(dve, ("oproj", q - 1, s))
                    nc.vector.tensor_tensor(gated[:, d, h, tok(s)], scratch(item), zs[:, h, tok(s)],
                                            ALU.mult).then_inc(s_read[BANK[item][0]], 1)
                elif stage == "add_attn":
                    q, r = a
                    lo, hi = ln_parts(2, q)[r]
                    normed_ready(dve, 2, q, hi // BPS - 1)
                    dve.wait_ge(s_x1in, 16 * (q + 1))
                    nc.vector.tensor_tensor(x1_of[q][:, lo:hi, :], x1_of[q][:, lo:hi, :],
                                            normed_of[q][:, lo:hi, :], ALU.add).then_inc(s_x1, 1)
                elif stage == "turn_x1" and a[0] == PAIRS - 1:
                    q, s = a
                    written(dve, item)
                    nc.vector.tensor_copy(x1_t[:, tok(s)], scratch(item)).then_inc(s_read[BANK[item][0]], 1)
                elif stage == "ffn_up":
                    q, s, c = a
                    if q == 0:
                        dve.wait_ge(s_hsilu, 3 * s + c + 1)
                    else:
                        was_read(dve, ("ffn_gate", q, s, c))
                    written(dve, item)
                    nc.vector.tensor_tensor(hid(s, c), scratch(item), hid(s, c),
                                            ALU.mult).then_inc(s_read[BANK[item][0]], 1)
                elif stage == "add_ffn":
                    q, r = a
                    lo, hi = ln_parts(4, q)[r]
                    normed_ready(dve, 4, q, hi // BPS - 1)
                    nc.vector.tensor_tensor(out_of[q][:, lo:hi, :], x1_of[q][:, lo:hi, :], normed_of[q][:, lo:hi, :],
                                            ALU.add).then_inc(s_x2, 1)


def kernel(**inputs):
    import numpy as np
    import concourse.bacc as bacc
    from concourse.bass_utils import run_bass_kernel_spmd

    w = {n[len("L0_"):]: np.asarray(a) for n, a in inputs.items()}
    dirs = ("attn_f_", "attn_b_")

    def halves(a):
        return a.reshape((2, P) + a.shape[1:])

    packed = np.zeros((P, NCOLS), np.float32)

    def put(name, a):
        packed[:, COLS[name][0]:COLS[name][1]] = a.reshape(P, -1)

    put("ident", np.eye(P, dtype=np.float32))
    put("rev", np.eye(P, dtype=np.float32)[::-1])
    put("gamma", w["attn_gamma"])
    put("beta", w["attn_beta"])
    for name, key in (("conv_b", "conv_b"), ("skip", "D"), ("a_log", "A_log")):
        put(name, np.stack([np.moveaxis(halves(w[d + key]), 1, 0) for d in dirs], 1))
    put("conv_w", w["attn_f_conv_w"][P:, 0, :])
    sel = np.zeros((P, NS), np.float32)
    for row in (ROW_HI, ROW_LO, ROW_MID):
        sel[row + np.arange(NS), np.arange(NS)] = 1
    put("sel", sel)
    put("wz", np.stack([w[d + "in_w"][DI:].T for d in dirs], 1))
    wx = np.zeros((P, 2, 2, XROWS), np.float32)
    for n, d in enumerate(dirs):
        xp = np.moveaxis(halves(w[d + "xproj_w"].T), 1, 0)
        for row in (ROW_HI, ROW_LO, ROW_MID):
            wx[:, n, :, row:row + NS] = xp[:, :, RANK:RANK + NS]
        wx[:, n, :, NS:2 * NS] = xp[:, :, RANK + NS:]
        wx[:, n, :, ROW_DT:XROWS] = xp[:, :, :RANK]
    put("wx", wx)
    put("wo", np.stack([np.moveaxis(halves(w[d + "out_w"].T), 1, 0) for d in dirs], 1))
    wdt = np.zeros((P, 2, DI), np.float32)
    for n, d in enumerate(dirs):
        wdt[ROW_DT:XROWS, n] = w[d + "dt_w"].T
        wdt[XROWS, n] = w[d + "dt_b"]
    put("wdt", wdt)
    taps = np.stack([np.broadcast_to(w[d + "conv_w"][:, 0, :].T, (P, TAPS, DI)) for d in dirs], 1)
    w_u = np.stack([w[d + "in_w"][:DI].T for d in dirs], 1)
    w_down = np.moveaxis(w["ffn_w_down"].T.reshape(3, P, DM), 1, 0).reshape(P, HID)
    w_ffn = np.concatenate([w["ffn_w_gate"].T, w["ffn_w_up"].T, w_down], 1)

    nc = bacc.Bacc("TRN2", target_bir_lowering=False, num_devices=1)
    arrays = {"x": w["attn_x"], "packed": packed, "conv_taps": taps, "w_u": w_u, "w_ffn": w_ffn}
    arrays = {n + "_dram": np.ascontiguousarray(a) for n, a in arrays.items()}
    args = [nc.dram_tensor(n, a.shape, mybir.dt.from_np(a.dtype), kind="ExternalInput").ap()
            for n, a in arrays.items()]
    args.append(nc.dram_tensor("c_rows_dram", (UNITS, NS, PT), F32, kind="Internal").ap())
    args.append(nc.dram_tensor("out_0_dram", (BATCH, SEQ, DM), F32, kind="ExternalOutput").ap())
    mamba_sandwich(nc, *args)
    r = run_bass_kernel_spmd(nc, [arrays], core_ids=[0])
    return r.results[0]["out_0_dram"]
```
